# Optimizing a Trainium2 kernel written in Bass

```python
import numpy as np
import jax
import jax.numpy as jnp

def _softmax(x, axis=-1):
    return jax.nn.softmax(x, axis=axis)

def _gelu(x):
    return jax.nn.gelu(x, approximate=True)

def _silu(x):
    return jax.nn.silu(x)

def _sigmoid(x):
    return jax.nn.sigmoid(x)

def _layernorm(x, axis=-1, eps=1e-05):
    m = jnp.mean(x, axis=axis, keepdims=True)
    v = jnp.var(x, axis=axis, keepdims=True)
    return (x - m) / jnp.sqrt(v + eps)

def _scatter_add(tgt, idx, src, axis=0):
    return tgt.at[idx].add(src)

def _segment_sum(src, seg, n):
    return jax.ops.segment_sum(src, seg, n)
kernel_name = 'mk_macaron_d1_jaxref_r4_e7730a'

def setup_inputs(seed: int=0):
    np.random.seed(seed)
    _w = jnp.asarray

    def _L0_attn_setup():
        import jax, jax.numpy as jnp
        import numpy as np
        D_MODEL = 256
        D_STATE = 16
        D_CONV = 4
        EXPAND = 2
        D_INNER = EXPAND * D_MODEL
        DT_RANK = (D_MODEL + 15) // 16
        BATCH = 4
        SEQ = 512

        def _layernorm(x, w, b):
            m = x.mean(-1, keepdims=True)
            v = ((x - m) ** 2).mean(-1, keepdims=True)
            return (x - m) * jax.lax.rsqrt(v + 1e-05) * w + b

        def _silu(x):
            return x * jax.nn.sigmoid(x)

        def _mamba_branch(xz, conv_w, conv_b, x_proj_w, dt_w, dt_b, A_log, D):
            x, z = jnp.split(xz, 2, axis=1)
            x = jax.lax.conv_general_dilated(x, conv_w, (1,), [(D_CONV - 1, 0)], dimension_numbers=('NCH', 'OIH', 'NCH'), feature_group_count=D_INNER) + conv_b[None, :, None]
            x = _silu(x)
            x_dbl = jnp.einsum('bdl,ed->bel', x, x_proj_w)
            dt, Bm, Cm = jnp.split(x_dbl, [DT_RANK, DT_RANK + D_STATE], axis=1)
            dt = jax.nn.softplus(jnp.einsum('brl,dr->bdl', dt, dt_w) + dt_b[None, :, None])
            A = -jnp.exp(A_log)

            def step(h, inp):
                dt_t, B_t, C_t, u_t = inp
                h = jnp.exp(dt_t[..., None] * A) * h + (dt_t * u_t)[..., None] * B_t[:, None, :]
                return (h, jnp.einsum('bdn,bn->bd', h, C_t))
            h0 = jnp.zeros((xz.shape[0], D_INNER, D_STATE), xz.dtype)
            _, ys = jax.lax.scan(step, h0, (dt.transpose(2, 0, 1), Bm.transpose(2, 0, 1), Cm.transpose(2, 0, 1), x.transpose(2, 0, 1)))
            y = ys.transpose(1, 2, 0) + D[None, :, None] * x
            return y * _silu(z)
        key = jax.random.key(seed)
        ks = jax.random.split(key, 16)

        def w(i, shape, s=0.02):
            return jax.random.normal(ks[i], shape, dtype=jnp.float32) * s
        A_init = jnp.log(jnp.broadcast_to(jnp.arange(1, D_STATE + 1, dtype=jnp.float32), (D_INNER, D_STATE)))
        return {'x': jax.random.normal(ks[0], (BATCH, SEQ, D_MODEL), dtype=jnp.float32), 'norm_w': jnp.ones((D_MODEL,), jnp.float32), 'norm_b': jnp.zeros((D_MODEL,), jnp.float32), 'in_proj_w': w(1, (2 * D_INNER, D_MODEL)), 'conv_w_f': w(2, (D_INNER, 1, D_CONV), 0.2), 'conv_b_f': jnp.zeros((D_INNER,), jnp.float32), 'x_proj_w_f': w(3, (DT_RANK + 2 * D_STATE, D_INNER)), 'dt_proj_w_f': w(4, (D_INNER, DT_RANK), 0.1), 'dt_proj_b_f': jnp.full((D_INNER,), -4.0, jnp.float32), 'A_log_f': A_init, 'D_f': jnp.ones((D_INNER,), jnp.float32), 'conv_w_r': w(5, (D_INNER, 1, D_CONV), 0.2), 'conv_b_r': jnp.zeros((D_INNER,), jnp.float32), 'x_proj_w_r': w(6, (DT_RANK + 2 * D_STATE, D_INNER)), 'dt_proj_w_r': w(7, (D_INNER, DT_RANK), 0.1), 'dt_proj_b_r': jnp.full((D_INNER,), -4.0, jnp.float32), 'A_log_r': A_init, 'D_r': jnp.ones((D_INNER,), jnp.float32), 'out_proj_w': w(8, (D_MODEL, D_INNER))}
    _L0_attn_in = _L0_attn_setup()

    def _L0_ffn_setup():
        import jax, jax.numpy as jnp
        import numpy as np
        N_HEADS = 16
        N_KV_HEADS = 4
        N_EMBD = 256
        HEAD_DIM = N_EMBD // N_HEADS
        N_EXPERTS = 8
        TOP_K = 2
        EPS = 1e-06

        def _rmsnorm(x, w):
            xf = x.astype(jnp.float32)
            n = xf * jax.lax.rsqrt(jnp.mean(xf * xf, axis=-1, keepdims=True) + EPS)
            return n.astype(x.dtype) * w

        def _gqa(x, wq, wk, wv, wo):
            B, S, C = x.shape
            n_rep = N_HEADS // N_KV_HEADS
            q = (x @ wq.T).reshape(B, S, N_HEADS, HEAD_DIM)
            k = (x @ wk.T).reshape(B, S, N_KV_HEADS, HEAD_DIM)
            v = (x @ wv.T).reshape(B, S, N_KV_HEADS, HEAD_DIM)
            k = jnp.repeat(k, n_rep, axis=2)
            v = jnp.repeat(v, n_rep, axis=2)
            scale = 1.0 / np.sqrt(HEAD_DIM).astype(np.float32)
            attn = jnp.einsum('bqhd,bkhd->bhqk', q, k) * scale
            causal = jnp.tril(jnp.ones((S, S), dtype=bool))
            attn = jnp.where(causal, attn, jnp.float32(-jnp.inf))
            attn = jax.nn.softmax(attn, axis=-1)
            out = jnp.einsum('bhqk,bkhd->bqhd', attn, v).reshape(B, S, C)
            return out @ wo.T

        def _moe(x, gate_w, expert_w):
            B, S, C = x.shape
            t = x.reshape(B * S, C)
            logits = t @ gate_w.T
            w, sel = jax.lax.top_k(logits, TOP_K)
            w = jax.nn.softmax(w.astype(jnp.float32), axis=1).astype(t.dtype)
            comb = jnp.sum(w[..., None] * jax.nn.one_hot(sel, N_EXPERTS, dtype=t.dtype), axis=1)
            out = jnp.zeros_like(t)
            for e in range(N_EXPERTS):
                out = out + comb[:, e, None] * (t @ expert_w[e].T)
            return out.reshape(B, S, C)
        key = jax.random.key(seed)
        ks = jax.random.split(key, 10)
        B, S, C = (4, 512, N_EMBD)
        s = 0.02
        return {'x': jax.random.normal(ks[0], (B, S, C), dtype=jnp.float32), 'attn_norm_w': jnp.ones((C,), dtype=jnp.float32), 'ffn_norm_w': jnp.ones((C,), dtype=jnp.float32), 'wq': jax.random.normal(ks[1], (C, C), dtype=jnp.float32) * s, 'wk': jax.random.normal(ks[2], (N_KV_HEADS * HEAD_DIM, C), dtype=jnp.float32) * s, 'wv': jax.random.normal(ks[3], (N_KV_HEADS * HEAD_DIM, C), dtype=jnp.float32) * s, 'wo': jax.random.normal(ks[4], (C, C), dtype=jnp.float32) * s, 'gate_w': jax.random.normal(ks[5], (N_EXPERTS, C), dtype=jnp.float32) * s, 'expert_w': jax.random.normal(ks[6], (N_EXPERTS, C, C), dtype=jnp.float32) * s}
    _L0_ffn_in = _L0_ffn_setup()
    _d = {'L0_attn_x': _L0_attn_in['x'], 'L0_attn_norm_w': _L0_attn_in['norm_w'], 'L0_attn_norm_b': _L0_attn_in['norm_b'], 'L0_attn_in_proj_w': _L0_attn_in['in_proj_w'], 'L0_attn_conv_w_f': _L0_attn_in['conv_w_f'], 'L0_attn_conv_b_f': _L0_attn_in['conv_b_f'], 'L0_attn_x_proj_w_f': _L0_attn_in['x_proj_w_f'], 'L0_attn_dt_proj_w_f': _L0_attn_in['dt_proj_w_f'], 'L0_attn_dt_proj_b_f': _L0_attn_in['dt_proj_b_f'], 'L0_attn_A_log_f': _L0_attn_in['A_log_f'], 'L0_attn_D_f': _L0_attn_in['D_f'], 'L0_attn_conv_w_r': _L0_attn_in['conv_w_r'], 'L0_attn_conv_b_r': _L0_attn_in['conv_b_r'], 'L0_attn_x_proj_w_r': _L0_attn_in['x_proj_w_r'], 'L0_attn_dt_proj_w_r': _L0_attn_in['dt_proj_w_r'], 'L0_attn_dt_proj_b_r': _L0_attn_in['dt_proj_b_r'], 'L0_attn_A_log_r': _L0_attn_in['A_log_r'], 'L0_attn_D_r': _L0_attn_in['D_r'], 'L0_attn_out_proj_w': _L0_attn_in['out_proj_w'], 'L0_ffn_attn_norm_w': _L0_ffn_in['attn_norm_w'], 'L0_ffn_ffn_norm_w': _L0_ffn_in['ffn_norm_w'], 'L0_ffn_wq': _L0_ffn_in['wq'], 'L0_ffn_wk': _L0_ffn_in['wk'], 'L0_ffn_wv': _L0_ffn_in['wv'], 'L0_ffn_wo': _L0_ffn_in['wo'], 'L0_ffn_gate_w': _L0_ffn_in['gate_w'], 'L0_ffn_expert_w': _L0_ffn_in['expert_w']}
    _x0 = _d['L0_attn_x']
    _d['L0_attn_x'] = jax.random.normal(jax.random.fold_in(jax.random.key(seed), 1), (4, 2048, 256), dtype=_x0.dtype)
    del _x0
    return _d

def reference(L0_attn_x, L0_attn_norm_w, L0_attn_norm_b, L0_attn_in_proj_w, L0_attn_conv_w_f, L0_attn_conv_b_f, L0_attn_x_proj_w_f, L0_attn_dt_proj_w_f, L0_attn_dt_proj_b_f, L0_attn_A_log_f, L0_attn_D_f, L0_attn_conv_w_r, L0_attn_conv_b_r, L0_attn_x_proj_w_r, L0_attn_dt_proj_w_r, L0_attn_dt_proj_b_r, L0_attn_A_log_r, L0_attn_D_r, L0_attn_out_proj_w, L0_ffn_attn_norm_w, L0_ffn_ffn_norm_w, L0_ffn_wq, L0_ffn_wk, L0_ffn_wv, L0_ffn_wo, L0_ffn_gate_w, L0_ffn_expert_w):

    def _L0_attn_ref(x, norm_w, norm_b, in_proj_w, conv_w_f, conv_b_f, x_proj_w_f, dt_proj_w_f, dt_proj_b_f, A_log_f, D_f, conv_w_r, conv_b_r, x_proj_w_r, dt_proj_w_r, dt_proj_b_r, A_log_r, D_r, out_proj_w):
        import jax, jax.numpy as jnp
        import numpy as np
        D_MODEL = 256
        D_STATE = 16
        D_CONV = 4
        EXPAND = 2
        D_INNER = EXPAND * D_MODEL
        DT_RANK = (D_MODEL + 15) // 16
        BATCH = 4
        SEQ = 512

        def _layernorm(x, w, b):
            m = x.mean(-1, keepdims=True)
            v = ((x - m) ** 2).mean(-1, keepdims=True)
            return (x - m) * jax.lax.rsqrt(v + 1e-05) * w + b

        def _silu(x):
            return x * jax.nn.sigmoid(x)

        def _mamba_branch(xz, conv_w, conv_b, x_proj_w, dt_w, dt_b, A_log, D):
            x, z = jnp.split(xz, 2, axis=1)
            x = jax.lax.conv_general_dilated(x, conv_w, (1,), [(D_CONV - 1, 0)], dimension_numbers=('NCH', 'OIH', 'NCH'), feature_group_count=D_INNER) + conv_b[None, :, None]
            x = _silu(x)
            x_dbl = jnp.einsum('bdl,ed->bel', x, x_proj_w)
            dt, Bm, Cm = jnp.split(x_dbl, [DT_RANK, DT_RANK + D_STATE], axis=1)
            dt = jax.nn.softplus(jnp.einsum('brl,dr->bdl', dt, dt_w) + dt_b[None, :, None])
            A = -jnp.exp(A_log)

            def step(h, inp):
                dt_t, B_t, C_t, u_t = inp
                h = jnp.exp(dt_t[..., None] * A) * h + (dt_t * u_t)[..., None] * B_t[:, None, :]
                return (h, jnp.einsum('bdn,bn->bd', h, C_t))
            h0 = jnp.zeros((xz.shape[0], D_INNER, D_STATE), xz.dtype)
            _, ys = jax.lax.scan(step, h0, (dt.transpose(2, 0, 1), Bm.transpose(2, 0, 1), Cm.transpose(2, 0, 1), x.transpose(2, 0, 1)))
            y = ys.transpose(1, 2, 0) + D[None, :, None] * x
            return y * _silu(z)
        h = _layernorm(x, norm_w, norm_b)
        xz = jnp.einsum('bld,ed->bel', h, in_proj_w)
        y_f = _mamba_branch(xz, conv_w_f, conv_b_f, x_proj_w_f, dt_proj_w_f, dt_proj_b_f, A_log_f, D_f)
        y_r = _mamba_branch(xz[..., ::-1], conv_w_r, conv_b_r, x_proj_w_r, dt_proj_w_r, dt_proj_b_r, A_log_r, D_r)[..., ::-1]
        out = jnp.einsum('bdl,od->blo', y_f + y_r, out_proj_w)
        return x + out

    def _L0_ffn_ref(x, attn_norm_w, ffn_norm_w, wq, wk, wv, wo, gate_w, expert_w):
        import jax, jax.numpy as jnp
        import numpy as np
        N_HEADS = 16
        N_KV_HEADS = 4
        N_EMBD = 256
        HEAD_DIM = N_EMBD // N_HEADS
        N_EXPERTS = 8
        TOP_K = 2
        EPS = 1e-06

        def _rmsnorm(x, w):
            xf = x.astype(jnp.float32)
            n = xf * jax.lax.rsqrt(jnp.mean(xf * xf, axis=-1, keepdims=True) + EPS)
            return n.astype(x.dtype) * w

        def _gqa(x, wq, wk, wv, wo):
            B, S, C = x.shape
            n_rep = N_HEADS // N_KV_HEADS
            q = (x @ wq.T).reshape(B, S, N_HEADS, HEAD_DIM)
            k = (x @ wk.T).reshape(B, S, N_KV_HEADS, HEAD_DIM)
            v = (x @ wv.T).reshape(B, S, N_KV_HEADS, HEAD_DIM)
            k = jnp.repeat(k, n_rep, axis=2)
            v = jnp.repeat(v, n_rep, axis=2)
            scale = 1.0 / np.sqrt(HEAD_DIM).astype(np.float32)
            attn = jnp.einsum('bqhd,bkhd->bhqk', q, k) * scale
            causal = jnp.tril(jnp.ones((S, S), dtype=bool))
            attn = jnp.where(causal, attn, jnp.float32(-jnp.inf))
            attn = jax.nn.softmax(attn, axis=-1)
            out = jnp.einsum('bhqk,bkhd->bqhd', attn, v).reshape(B, S, C)
            return out @ wo.T

        def _moe(x, gate_w, expert_w):
            B, S, C = x.shape
            t = x.reshape(B * S, C)
            logits = t @ gate_w.T
            w, sel = jax.lax.top_k(logits, TOP_K)
            w = jax.nn.softmax(w.astype(jnp.float32), axis=1).astype(t.dtype)
            comb = jnp.sum(w[..., None] * jax.nn.one_hot(sel, N_EXPERTS, dtype=t.dtype), axis=1)
            out = jnp.zeros_like(t)
            for e in range(N_EXPERTS):
                out = out + comb[:, e, None] * (t @ expert_w[e].T)
            return out.reshape(B, S, C)
        h = x + _gqa(_rmsnorm(x, attn_norm_w), wq, wk, wv, wo)
        out = h + _moe(_rmsnorm(h, ffn_norm_w), gate_w, expert_w)
        return out
    x = L0_attn_x
    x = x + 0.5 * _L0_ffn_ref(_layernorm(x, axis=-1), L0_ffn_attn_norm_w, L0_ffn_ffn_norm_w, L0_ffn_wq, L0_ffn_wk, L0_ffn_wv, L0_ffn_wo, L0_ffn_gate_w, L0_ffn_expert_w)
    x = x + _L0_attn_ref(_layernorm(x, axis=-1), L0_attn_norm_w, L0_attn_norm_b, L0_attn_in_proj_w, L0_attn_conv_w_f, L0_attn_conv_b_f, L0_attn_x_proj_w_f, L0_attn_dt_proj_w_f, L0_attn_dt_proj_b_f, L0_attn_A_log_f, L0_attn_D_f, L0_attn_conv_w_r, L0_attn_conv_b_r, L0_attn_x_proj_w_r, L0_attn_dt_proj_w_r, L0_attn_dt_proj_b_r, L0_attn_A_log_r, L0_attn_D_r, L0_attn_out_proj_w)
    x = x + 0.5 * _L0_ffn_ref(_layernorm(x, axis=-1), L0_ffn_attn_norm_w, L0_ffn_ffn_norm_w, L0_ffn_wq, L0_ffn_wk, L0_ffn_wv, L0_ffn_wo, L0_ffn_gate_w, L0_ffn_expert_w)
    return x

_drawn_inputs = setup_inputs


def setup_inputs(seed=0):
    import zlib

    import numpy as np

    out = dict(_drawn_inputs(seed))
    spreads = {'L0_attn_norm_w': (1.0, 0.2),
     'L0_attn_norm_b': (0.0, 0.1),
     'L0_attn_conv_b_f': (0.0, 0.1),
     'L0_attn_dt_proj_b_f': (-4.0, 0.2),
     'L0_attn_D_f': (1.0, 0.2),
     'L0_attn_conv_b_r': (0.0, 0.1),
     'L0_attn_dt_proj_b_r': (-4.0, 0.2),
     'L0_attn_D_r': (1.0, 0.2),
     'L0_ffn_attn_norm_w': (1.0, 0.2),
     'L0_ffn_ffn_norm_w': (1.0, 0.2)}
    factors = {}
    for name, (base, spread) in spreads.items():
        noise = np.random.default_rng([zlib.crc32(name.encode()), seed]).standard_normal(out[name].shape)
        drawn = base * np.exp(spread * noise) if base else spread * noise
        out[name] = jnp.asarray(drawn.astype(out[name].dtype))
    for name, factor in factors.items():
        out[name] = (out[name] * factor).astype(out[name].dtype)
    return out
```

```python
import concourse.bass as bass
from concourse import mybir
from contextlib import ExitStack

F32 = mybir.dt.float32
BF16 = mybir.dt.bfloat16
ALU = mybir.AluOpType
ACT = mybir.ActivationFunctionType
AX = mybir.AxisListType

P = 128
C = 256
CK = C // P
CH = 512
TT = CH // P
HEADS, KVH, HD = 16, 4, 16
REP = HEADS // KVH
KW = KVH * HD
NE = 8
DI, DS, DTR = 512, 16, 16
DM = DI // P
TAPS = 4
HALO = TAPS - 1
WIN = CH + 2 * HALO
UNITS = DM * DS


class Phase:

    def __init__(self, nc, tag):
        self.nc, self.tag, self.ctx, self.sems = nc, tag, ExitStack(), []

    def __enter__(self):
        return self

    def sb(self, name, shape, dtype=F32):
        return self.ctx.enter_context(self.nc.sbuf_tensor(f"{self.tag}_{name}", shape, dtype))

    def sem(self, name):
        self.sems.append(self.nc.alloc_semaphore(f"{self.tag}_{name}"))
        return self.sems[-1]

    def __exit__(self, *exc):
        if exc[0] is None:
            self.nc.clear_and_free_semaphores(self.sems)
            self.nc.all_engine_barrier()
            self.ctx.close()
        return False


def looped(eng, n, body):
    if n > 1:
        with eng.Fori(0, n - 1) as i:
            body(i, False)
    body(n - 1, True)


def hold(eng, sem, value, passed):
    eng.wait_ge(sem, value)
    eng.sem_inc(passed, 1)


def rows(ap, i):
    return ap[bass.ds(i * CH, CH), :].rearrange("(t p) c -> p t c", p=P)


def cols(ap, i):
    return ap[:, bass.ds(i * CH, CH)].rearrange("(m p) t -> p m t", p=P)


def make_constants(nc, ident):
    with Phase(nc, "const") as ph:
        made = ph.sem("made")
        with nc.Block() as block:
            @block.gpsimd
            def _(pool):
                nc.gpsimd.memset(ident[:, :], 0.0).then_inc(made, 1)
                pool.wait_ge(made, 1)
                nc.gpsimd.affine_select(out=ident[:, :], in_=ident[:, :], compare_op=ALU.not_equal, fill=1.0,
                                        base=0, pattern=[[-1, P]], channel_multiplier=1).then_inc(made, 1)
                pool.wait_ge(made, 2)


def ffn_in(nc, tag, psum, ident, x, t_out, qp, kp, v_out, w_norm, wqT, wkT, wvT, B, S):
    NC = S // CH
    n_chunks = B * NC
    STORES = 16 * (TT + 3 * (CK + 1))
    with Phase(nc, tag) as ph:
        sb, sem = ph.sb, ph.sem
        xs = sb("xs", [P, TT, C])
        tn = sb("tn", [P, TT, C])
        an = sb("an", [P, TT, C])
        aT = sb("aT", [P, CK, CH])
        wn = sb("wn", [P, CK])
        wq = sb("wq", [P, CK, C])
        wk = sb("wk", [P, CK, KW])
        wv = sb("wv", [P, CK, KW])
        st6 = sb("st6", [P, TT, 6])
        mv = sb("mv", [P, TT, 2])
        va, vb, vc = (sb(n, [P, TT]) for n in ("va", "vb", "vc"))
        rq = sb("rq", [P, 2, TT])
        rs = sb("rs", [P, 2, TT])
        q3 = sb("q3", [P, 3, CK, CH], BF16)
        k3 = sb("k3", [KW, 3, CH], BF16)
        qr = sb("qr", [P, CK, CH])
        kr = sb("kr", [KW, CH])
        vs = sb("vs", [P, TT, KW])
        w_in, x_in = sem("w_in"), sem("x_in")
        stats, small, inv_vars, roots = sem("stats"), sem("small"), sem("inv_vars"), sem("roots")
        dve_passed, sp_passed = sem("dve_passed"), sem("sp_passed")
        t_ready, t_stored, a_ready = sem("t_ready"), sem("t_stored"), sem("a_ready")
        aT_ps, aT_sb, q_ps, k_ps, v_ps = sem("aT_ps"), sem("aT_sb"), sem("q_ps"), sem("k_ps"), sem("v_ps")
        high, rest, mid, low, v_ready = sem("high"), sem("rest"), sem("mid"), sem("low"), sem("v_ready")
        stored = sem("stored")

        with nc.Block() as block:
            @block.sync
            def _(sp):
                sp.dma_start(xs[:, :, :], rows(x, 0)).then_inc(x_in, 16)
                sp.dma_start(wq[:, :, :], wqT.rearrange("(k p) n -> p k n", p=P)).then_inc(w_in, 16)
                sp.dma_start(wk[:, :, :], wkT.rearrange("(k p) n -> p k n", p=P)).then_inc(w_in, 16)
                sp.dma_start(wv[:, :, :], wvT.rearrange("(k p) n -> p k n", p=P)).then_inc(w_in, 16)
                sp.dma_start(wn[:, :], w_norm).then_inc(w_in, 16)

                def chunk(i, last):
                    if not last:
                        sp.wait_ge(t_ready, TT * (i + 1))
                        sp.dma_start(xs[:, :, :], rows(x, i + 1)).then_inc(x_in, 16)
                    sp.wait_ge(t_ready, TT * (i + 1))
                    sp.dma_start(rows(t_out, i), tn[:, :, :]).then_inc(t_stored, 16)
                    sp.wait_ge(v_ready, i + 1)
                    b, token = i // NC, bass.ds((i % NC) * CH, CH)
                    for t in range(TT):
                        sp.dma_start(v_out[bass.ds(b * KVH, KVH), bass.ds((i % NC) * CH + t * P, P), :]
                                     .rearrange("g p d -> p g d"),
                                     vs[:, t, :].rearrange("p (g d) -> p g d", g=KVH)).then_inc(stored, 16)
                    for part, done in enumerate((high, mid, low)):
                        sp.wait_ge(done, 2 * (i + 1))
                        for m in range(CK):
                            heads = bass.ds(b * HEADS + m * (P // HD), P // HD)
                            sp.dma_start(qp[heads, part, :, token], q3[:, part, m, :]).then_inc(stored, 16)
                        sp.dma_start(kp[bass.ds(b * KVH, KVH), part, :, token], k3[:, part, :]).then_inc(stored, 16)
                looped(sp, n_chunks, chunk)
                sp.wait_ge(t_stored, 16 * n_chunks)
                sp.wait_ge(stored, STORES * n_chunks)

            @block.vector
            def _(dve):
                def norm(i):
                    dve.wait_ge(x_in, 16 * (i + 1))
                    for t in range(TT):
                        nc.vector.bn_stats(st6[:, t, :], xs[:, t, :]).then_inc(stats, 1)
                    hold(dve, stats, 2 * TT * i + TT, dve_passed)
                    for t in range(TT):
                        nc.vector.bn_aggr(mv[:, t, :], st6[:, t, :]).then_inc(stats, 1)
                    dve.wait_ge(stats, 2 * TT * (i + 1))
                    nc.vector.tensor_scalar(va[:, :], mv[:, :, 1], 1e-5, None, ALU.add).then_inc(small, 1)
                    dve.wait_ge(small, 4 * i + 1)
                    nc.vector.reciprocal(rq[:, 0, :], va[:, :]).then_inc(small, 1)
                    dve.wait_ge(small, 4 * i + 2)
                    nc.vector.tensor_tensor(vb[:, :], mv[:, :, 1], rq[:, 0, :], ALU.mult).then_inc(small, 1)
                    dve.wait_ge(small, 4 * i + 3)
                    nc.vector.tensor_scalar(vc[:, :], vb[:, :], 1e-6, None, ALU.add).then_inc(small, 1)
                    dve.wait_ge(small, 4 * i + 4)
                    nc.vector.reciprocal(rq[:, 1, :], vc[:, :]).then_inc(inv_vars, 1)
                    dve.wait_ge(roots, i + 1)
                    dve.wait_ge(t_stored, 16 * i)
                    for t in range(TT):
                        nc.vector.tensor_scalar(tn[:, t, :], xs[:, t, :], mv[:, t, 0:1], rs[:, 0, t:t + 1],
                                                ALU.subtract, ALU.mult).then_inc(t_ready, 1)
                    dve.wait_ge(aT_ps, i)
                    for t in range(TT):
                        dve.wait_ge(t_ready, TT * i + t + 1)
                        nc.vector.tensor_scalar(an[:, t, :], tn[:, t, :], rs[:, 1, t:t + 1], None,
                                                ALU.mult).then_inc(a_ready, 1)

                def split(i):
                    dve.wait_ge(q_ps, i + 1)
                    dve.wait_ge(high, 2 * i + 1)
                    nc.vector.tensor_tensor(qr[:, :, :], psum[:, 2:4, :], q3[:, 0, :, :], ALU.subtract).then_inc(rest, 1)
                    dve.wait_ge(high, 2 * i + 2)
                    nc.vector.tensor_tensor(kr[:, :], psum[0:KW, 4, :], k3[:, 0, :], ALU.subtract).then_inc(rest, 1)
                    dve.wait_ge(stored, STORES * i)
                    dve.wait_ge(mid, 2 * i + 1)
                    nc.vector.tensor_tensor(q3[:, 2, :, :], qr[:, :, :], q3[:, 1, :, :], ALU.subtract).then_inc(low, 1)
                    dve.wait_ge(mid, 2 * i + 2)
                    nc.vector.tensor_tensor(k3[:, 2, :], kr[:, :], k3[:, 1, :], ALU.subtract).then_inc(low, 1)

                norm(0)

                def chunk(i, last):
                    if not last:
                        norm(i + 1)
                    split(i)
                looped(dve, n_chunks, chunk)

            @block.tensor
            def _(pe):
                pe.wait_ge(w_in, 64)

                def chunk(i, last):
                    pe.wait_ge(aT_sb, CK * i)
                    for t in range(TT):
                        pe.wait_ge(a_ready, TT * i + t + 1)
                        for k in range(CK):
                            ins = nc.tensor.transpose(psum[:, k, t * P:(t + 1) * P], an[:, t, k * P:(k + 1) * P],
                                                      ident[:, :])
                    ins.then_inc(aT_ps, 1)
                    pe.wait_ge(aT_sb, CK * (i + 1))
                    pe.wait_ge(rest, 2 * i)
                    pe.wait_ge(v_ready, i)
                    for m in range(CK):
                        for k in range(CK):
                            ins = nc.tensor.matmul(psum[:, 2 + m, :], wq[:, k, m * P:(m + 1) * P], aT[:, k, :],
                                                   start=k == 0, stop=k == CK - 1)
                    ins.then_inc(q_ps, 1)
                    for k in range(CK):
                        ins = nc.tensor.matmul(psum[0:KW, 4, :], wk[:, k, :], aT[:, k, :],
                                               start=k == 0, stop=k == CK - 1)
                    ins.then_inc(k_ps, 1)
                    for t in range(TT):
                        for k in range(CK):
                            ins = nc.tensor.matmul(psum[:, 5, t * KW:(t + 1) * KW], aT[:, k, t * P:(t + 1) * P],
                                                   wv[:, k, :], start=k == 0, stop=k == CK - 1)
                    ins.then_inc(v_ps, 1)
                looped(pe, n_chunks, chunk)

            @block.scalar
            def _(act):
                act.wait_ge(w_in, 64)

                def root(i):
                    act.wait_ge(inv_vars, i + 1)
                    act.wait_ge(a_ready, TT * i)
                    nc.scalar.activation(rs[:, :, :], rq[:, :, :], ACT.Sqrt).then_inc(roots, 1)

                def chunk(i, last):
                    act.wait_ge(aT_ps, i + 1)
                    act.wait_ge(v_ps, i)
                    for k in range(CK):
                        nc.scalar.activation(aT[:, k, :], psum[:, k, :], ACT.Copy, scale=wn[:, k:k + 1]).then_inc(aT_sb, 1)
                    if not last:
                        root(i + 1)
                    act.wait_ge(q_ps, i + 1)
                    act.wait_ge(stored, STORES * i)
                    nc.scalar.activation(q3[:, 0, :, :], psum[:, 2:4, :], ACT.Copy).then_inc(high, 1)
                    act.wait_ge(k_ps, i + 1)
                    nc.scalar.activation(k3[:, 0, :], psum[0:KW, 4, :], ACT.Copy).then_inc(high, 1)
                    act.wait_ge(v_ps, i + 1)
                    nc.scalar.activation(vs[:, :, :], psum[:, 5, 0:TT * KW].rearrange("p (t n) -> p t n", n=KW),
                                         ACT.Copy).then_inc(v_ready, 1)
                    act.wait_ge(rest, 2 * i + 1)
                    nc.scalar.activation(q3[:, 1, :, :], qr[:, :, :], ACT.Copy).then_inc(mid, 1)
                    act.wait_ge(rest, 2 * i + 2)
                    nc.scalar.activation(k3[:, 1, :], kr[:, :], ACT.Copy).then_inc(mid, 1)
                root(0)
                looped(act, n_chunks, chunk)


PARTS = 6 * HD
SROWS = PARTS + 3
VW = 32
NEG = -3.0e38


def attention(nc, tag, psum, ident, qp, kp, v_in, ao, B, S):
    NT_Q = S // P
    NQB = S // CH
    N = B * KVH
    MROWS = REP * NT_Q
    blocks = [(qb, kb) for qb in range(NQB) for kb in range(TT * (qb + 1))]
    pieces = [(i, h, c) for i in range(NT_Q) for h in range(REP) for c in range(0, i + 1, TT)]
    NB, NP = len(blocks), len(pieces)
    share = [pieces[NP * s // NB:NP * (s + 1) // NB] for s in range(NB)]
    before = [NP * s // NB for s in range(NB)]
    PB = 3
    E0, PV0 = 1, PB - 1

    def closes(s):
        return s >= 0 and blocks[s][1] == TT * (blocks[s][0] + 1) - 1

    def diag(s):
        qb, kb = blocks[s]
        return kb - TT * qb

    with Phase(nc, tag) as ph:
        sb, sem = ph.sb, ph.sem
        Q = [sb(f"q{p}", [SROWS, REP, S], BF16) for p in range(2)]
        K = [sb(f"k{p}", [SROWS, S], BF16) for p in range(2)]
        V = [sb(f"v{p}", [P, S // P, VW]) for p in range(2)]
        E = sb("e", [P, PB, REP, CH])
        O = sb("o", [P, CH])
        on = sb("on", [P, TT, REP, HD])
        rec = sb("rec", [P, TT, REP])
        mask = sb("mask", [P, P], BF16)
        identb = sb("identb", [P, P], BF16)
        mx = sb("mx", [P, MROWS, NQB])
        nm = sb("nm", [P, MROWS])
        m3 = sb("m3", [MROWS, 3, P], BF16)
        mr = sb("mr", [MROWS, P])
        made, loaded = sem("made"), [sem("loaded_even"), sem("loaded_odd")]
        m_ps, m_red, n_max, mT_ps = sem("m_ps"), sem("m_red"), sem("n_max"), sem("mT_ps")
        m_high, m_rest, m_mid, m_low, m_in = sem("m_high"), sem("m_rest"), sem("m_mid"), sem("m_low"), sem("m_in")
        pool_passed, pe_passed = sem("pool_passed"), sem("pe_passed")
        s_ps, e_ready, masked, pv = sem("s_ps"), sem("e_ready"), sem("masked"), sem("pv")
        o_sb, oT_ps, recip, normed, stored = sem("o_sb"), sem("oT_ps"), sem("recip"), sem("normed"), sem("stored")
        BANK_O, BANK_M, BANK_T = 4, 5, 7

        def phase_steps(eng, step):
            if N > 2:
                with eng.Fori(0, N // 2 - 1) as j:
                    step(j * 2, 0, True, True)
                    step(j * 2 + 1, 1, True, True)
            step(N - 2, 0, True, False)
            step(N - 1, 1, False, False)

        with nc.Block() as block:
            @block.sync
            def _(sp):
                def load(it, par):
                    b, g = it // KVH, it % KVH
                    q, k, v = Q[par], K[par], V[par]
                    row = 0
                    for n in (3, 2, 1):
                        src = qp[bass.ds(it * REP, REP), 0:n, :, :]
                        sp.dma_start(q[row:row + n * HD, :, :], src.rearrange("h p d t -> (p d) h t")).then_inc(loaded[par], 16)
                        for r in range(n):
                            sp.dma_start(k[row + r * HD:row + (r + 1) * HD, :],
                                         kp[bass.ds(it, 1), 3 - n, :, :].rearrange("o d t -> (o d) t")).then_inc(loaded[par], 16)
                        row += n * HD
                    sp.dma_start(v[:, :, 0:HD], v_in[bass.ds(it, 1), :, :].rearrange("o (n p) d -> p (o n) d", p=P)
                                 ).then_inc(loaded[par], 16)

                def put_maxima(it, par):
                    for p_ in range(3):
                        sp.wait_ge((m_high, m_mid, m_low)[p_], it + 1)
                        sp.dma_start(Q[par][PARTS + p_:PARTS + p_ + 1, :, :], m3[:, p_, :]).then_inc(m_in, 16)

                sp.wait_ge(made, 9)
                load(0, 0)
                load(1, 1)
                put_maxima(0, 0)

                def step(it, par, nxt, ld):
                    b, g = it // KVH, it % KVH
                    for qb in range(NQB):
                        sp.wait_ge(normed, it * NQB + qb + 1)
                        sp.dma_start(ao[bass.ds(b * S + qb * CH, CH), bass.ds(g * REP * HD, REP * HD)]
                                     .rearrange("(t p) c -> p t c", p=P),
                                     on[:, :, :, :].rearrange("p t h d -> p t (h d)")).then_inc(stored, 16)
                    if nxt:
                        put_maxima(it + 1, 1 - par)
                    if ld:
                        sp.wait_ge(pv, PV0 + (it + 1) * NB)
                        load(it + 2, par)
                phase_steps(sp, step)
                sp.wait_ge(stored, 16 * NQB * N)

            @block.gpsimd
            def _(pool):
                pool.wait_ge(made, 8)
                nc.gpsimd.affine_select(out=mask[:, :], in_=mask[:, :], compare_op=ALU.is_ge, fill=NEG, base=0,
                                        pattern=[[-1, P]], channel_multiplier=1).then_inc(made, 1)

                def step(it, par, nxt, ld):
                    for s in range(NB):
                        if diag(s) >= 0:
                            off = diag(s) * P
                            hold(pool, e_ready, E0 + 2 * (it * NB + s + 1), pool_passed)
                            part = E[:, s % PB, :, off:off + P]
                            nc.gpsimd.affine_select(out=part, in_=part, compare_op=ALU.is_ge, fill=0.0, base=0,
                                                    pattern=[[0, REP], [1, P]], channel_multiplier=-1).then_inc(masked, 1)
                phase_steps(pool, step)

            @block.tensor
            def _(pe):
                pe.sem_inc(pv, PV0)
                pe.wait_ge(made, 9)

                def maxima(it, par, first, todo):
                    q, k = Q[par], K[par]
                    if first == 0:
                        pe.wait_ge(loaded[par], 160 * (it // 2 + 1))
                    for n, (i, h, c) in enumerate(todo, first):
                        if not (isinstance(it, int) and it == 0 and n < 2):
                            pe.wait_ge(m_red, it * NP + n - 1)
                        w = min(TT, i + 1 - c) * P
                        bank = psum[:, BANK_M + n % 2, :]
                        is_diag = c + TT > i
                        ins = nc.tensor.matmul(bank[:, 0:w], q[0:PARTS, h, i * P:(i + 1) * P], k[0:PARTS, c * P:c * P + w],
                                               start=True, stop=not is_diag)
                        if is_diag:
                            ins = nc.tensor.matmul(bank[:, w - P:w], identb[:, :], mask[:, :], start=False, stop=True)
                        ins.then_inc(m_ps, 1)

                def turn_maxima(it):
                    hold(pe, n_max, it + 1, pe_passed)
                    nc.tensor.transpose(psum[0:MROWS, BANK_T, 0:P], nm[:, :], ident[:, :]).then_inc(mT_ps, 1)

                def weighted(it, par, s):
                    qb, kb = blocks[s]
                    off = max(diag(s), 0) * P
                    pe.wait_ge(e_ready, E0 + 2 * (it * NB + s + 1))
                    if diag(s) >= 0:
                        n_diag = sum(diag(z) >= 0 for z in range(s + 1))
                        pe.wait_ge(masked, it * NQB * TT + n_diag)
                    if kb == 0:
                        pe.wait_ge(o_sb, it * NQB + qb)
                    for h in range(REP):
                        ins = nc.tensor.matmul(psum[32 * h:32 * h + VW, BANK_O, off:CH], V[par][:, kb, :],
                                               E[:, s % PB, h, off:CH], start=kb == 0, stop=closes(s),
                                               tile_position=(0, 32 * h))
                    ins.then_inc(pv, 1)

                def turn_output(it, qb):
                    pe.wait_ge(o_sb, it * NQB + qb + 1)
                    pe.wait_ge(normed, it * NQB + qb)
                    for t in range(TT):
                        ins = nc.tensor.transpose(psum[:, BANK_T, t * P:(t + 1) * P], O[:, t * P:(t + 1) * P], ident[:, :])
                    ins.then_inc(oT_ps, 1)

                for s in range(NB):
                    maxima(0, 0, before[s], share[s])
                turn_maxima(0)

                def step(it, par, nxt, ld):
                    q, k = Q[par], K[par]
                    pe.wait_ge(m_in, 48 * (it + 1))
                    for s in range(NB):
                        qb, kb = blocks[s]
                        off = max(diag(s), 0) * P
                        for h in range(REP):
                            if h % 2 == 0:
                                pe.wait_ge(e_ready, E0 + 2 * (it * NB + s) + h // 2 - 1)
                            ins = nc.tensor.matmul(psum[:, h, off:CH], k[:, kb * P:(kb + 1) * P],
                                                   q[:, h, qb * CH + off:(qb + 1) * CH], start=True, stop=True)
                            if h % 2:
                                ins.then_inc(s_ps, 1)
                        if nxt:
                            maxima(it + 1, 1 - par, before[s], share[s])
                        if s > 0:
                            weighted(it, par, s - 1)
                        if closes(s - 2):
                            turn_output(it, blocks[s - 2][0])
                    weighted(it, par, NB - 1)
                    turn_output(it, NQB - 1)
                    if nxt:
                        pe.wait_ge(normed, (it + 1) * NQB)
                        turn_maxima(it + 1)
                phase_steps(pe, step)

            @block.scalar
            def _(act):
                def split(it):
                    act.wait_ge(mT_ps, it + 1)
                    act.wait_ge(m_in, 48 * it)
                    nc.scalar.activation(m3[:, 0, :], psum[0:MROWS, BANK_T, 0:P], ACT.Copy).then_inc(m_high, 1)
                    act.wait_ge(m_rest, it + 1)
                    nc.scalar.activation(m3[:, 1, :], mr[:, :], ACT.Copy).then_inc(m_mid, 1)

                act.sem_inc(e_ready, E0)
                split(0)

                def step(it, par, nxt, ld):
                    for s in range(NB):
                        off = max(diag(s), 0) * P
                        for hp in range(2):
                            act.wait_ge(s_ps, 2 * (it * NB + s) + hp + 1)
                            if hp == 0:
                                act.wait_ge(pv, PV0 + it * NB + s - PB + 1)
                            nc.scalar.activation(E[:, s % PB, 2 * hp:2 * hp + 2, off:CH], psum[:, 2 * hp:2 * hp + 2, off:CH],
                                                 ACT.Exp, scale=HD ** -0.5).then_inc(e_ready, 1)
                        if closes(s - 1):
                            output(it, s - 1)
                    output(it, NB - 1)
                    if nxt:
                        split(it + 1)

                def output(it, s):
                    qb = blocks[s][0]
                    act.wait_ge(pv, PV0 + it * NB + s + 1)
                    act.wait_ge(oT_ps, it * NQB + qb)
                    nc.scalar.activation(O[:, :], psum[:, BANK_O, :], ACT.Copy).then_inc(o_sb, 1)
                phase_steps(act, step)

            @block.vector
            def _(dve):
                for p in range(2):
                    nc.vector.memset(V[p][:, :, HD:VW], 0.0).then_inc(made, 1)
                    nc.vector.memset(K[p][PARTS:SROWS, :], 1.0).then_inc(made, 1)
                dve.wait_ge(made, 4)
                for p in range(2):
                    nc.vector.memset(V[p][:, :, HD:HD + 1], 1.0).then_inc(made, 1)
                nc.vector.memset(mask[:, :], 0.0).then_inc(made, 1)
                nc.vector.tensor_copy(identb[:, :], ident[:, :]).then_inc(made, 1)
                nc.vector.memset(mx[:, :, :], NEG).then_inc(recip, 1)

                def reduce(it, first, todo):
                    for n, (i, h, c) in enumerate(todo, first):
                        dve.wait_ge(m_ps, it * NP + n + 1)
                        if n == 0:
                            dve.wait_ge(n_max, it)
                        w = min(TT, i + 1 - c) * P
                        nc.vector.reduce_max(mx[:, h * NT_Q + i, c // TT:c // TT + 1], psum[:, BANK_M + n % 2, 0:w],
                                             AX.X).then_inc(m_red, 1)

                def negate(it):
                    dve.wait_ge(m_red, (it + 1) * NP)
                    dve.wait_ge(mT_ps, it)
                    nc.vector.tensor_reduce(nm[:, :], mx[:, :, :], AX.X, ALU.max, negate=True).then_inc(n_max, 1)

                def split(it):
                    dve.wait_ge(m_high, it + 1)
                    nc.vector.tensor_tensor(mr[:, :], psum[0:MROWS, BANK_T, 0:P], m3[:, 0, :], ALU.subtract).then_inc(m_rest, 1)
                    dve.wait_ge(m_mid, it + 1)
                    nc.vector.tensor_tensor(m3[:, 2, :], mr[:, :], m3[:, 1, :], ALU.subtract).then_inc(m_low, 1)

                def normalise(it, qb):
                    dve.wait_ge(oT_ps, it * NQB + qb + 1)
                    o = psum[:, BANK_T, :].rearrange("p (t h d) -> p t h d", t=TT, h=REP)
                    nc.vector.reciprocal(rec[:, :, :], o[:, :, :, HD]).then_inc(recip, 1)
                    dve.wait_ge(recip, it * NQB + qb + 2)
                    dve.wait_ge(stored, 16 * (it * NQB + qb))
                    nc.vector.tensor_tensor(on[:, :, :, :], o[:, :, :, 0:HD],
                                            rec[:, :, :].unsqueeze(3).to_broadcast([P, TT, REP, HD]), ALU.mult
                                            ).then_inc(normed, 1)
                dve.wait_ge(recip, 1)
                for s in range(NB):
                    reduce(0, before[s], share[s])
                negate(0)
                split(0)

                def step(it, par, nxt, ld):
                    for s in range(NB):
                        if nxt:
                            reduce(it + 1, before[s], share[s])
                        if closes(s - 2):
                            normalise(it, blocks[s - 2][0])
                    if nxt:
                        negate(it + 1)
                    normalise(it, NQB - 1)
                    if nxt:
                        split(it + 1)
                phase_steps(dve, step)


def ffn_out(nc, tag, psum, ident, ao, t_in, x, x_out, w_norm, woT, gateT, expT, n_chunks):
    NP = NE // 2
    GATE = 13
    ADDED0 = 6
    with Phase(nc, tag) as ph:
        sb, sem = ph.sb, ph.sem
        aos = sb("aos", [P, TT, C])
        ts = sb("ts", [P, TT, C])
        xs = [sb(f"xs{p}", [P, TT, C]) for p in range(2)]
        h = [sb(f"h{p}", [P, TT, C]) for p in range(2)]
        un = sb("un", [P, TT, C])
        aT = sb("aT", [P, CK, CH])
        uT = [sb(f"uT{p}", [P, CK, CH]) for p in range(2)]
        acc = sb("acc", [P, 2, C])
        res = sb("res", [P, TT, C])
        sq = sb("sq", [P, C])
        ss, va, ri, rs = (sb(n, [P, TT]) for n in ("ss", "va", "ri", "rs"))
        lg, ex, sel = (sb(n, [P, TT, NE]) for n in ("lg", "ex", "sel"))
        comb = [sb(f"comb{p}", [P, TT, NE]) for p in range(2)]
        gt, ge, gl, gu, above = (sb(n, [P, TT, NE, NE]) for n in ("gt", "ge", "gl", "gu", "above"))
        best, rank, den, rden = sb("best", [P, TT]), sb("rank", [P, TT, NE]), sb("den", [P, TT]), sb("rden", [P, TT])
        dl = sb("dl", [P, TT, NE])
        lower = sb("lower", [P, TT, NE, NE])
        upper = sb("upper", [P, TT, NE, NE])
        wn = sb("wn", [P, CK])
        wo = sb("wo", [P, CK, C])
        wg = sb("wg", [P, CK, NE])
        we = sb("we", [P, CK, NE, C])
        w_in, ones, masks, sp_passed = sem("w_in"), sem("ones"), sem("masks"), sem("sp_passed")
        at_in, x_in = sem("at_in"), [sem("x_in_even"), sem("x_in_odd")]
        aT_ps, aT_sb, o_ps, h_ready = sem("aT_ps"), sem("aT_sb"), sem("o_ps"), sem("h_ready")
        squares, inv_var, roots, small = sem("squares"), sem("inv_var"), sem("roots"), sem("small")
        u_ready, uT_ps, uT_sb, l_ps = sem("u_ready"), sem("uT_ps"), sem("uT_sb"), sem("l_ps")
        l_sb, gated, exps, comb_ready = sem("l_sb"), sem("gated"), sem("exps"), sem("comb_ready")
        e_ps, added, r_ready, stored = sem("e_ps"), sem("added"), sem("r_ready"), sem("stored")
        BANK_A, BANK_O, BANK_L, BANKS_E = 0, 2, 2, (4, 5, 6, 7)

        def phase_steps(eng, step):
            if n_chunks > 2:
                with eng.Fori(0, n_chunks // 2 - 1) as j:
                    step(j * 2, 0, True)
                    step(j * 2 + 1, 1, True)
            step(n_chunks - 2, 0, True)
            step(n_chunks - 1, 1, False)

        with nc.Block() as block:
            @block.sync
            def _(sp):
                def load(i, par, first=False):
                    if not first:
                        hold(sp, aT_ps, i, sp_passed)
                        hold(sp, h_ready, 2 * i, sp_passed)
                    sp.dma_start(aos[:, :, :], rows(ao, i)).then_inc(at_in, 16)
                    sp.dma_start(ts[:, :, :], rows(t_in, i)).then_inc(at_in, 16)
                    if not first:
                        sp.wait_ge(r_ready, TT * (i - 1))
                    sp.dma_start(xs[par][:, :, :], rows(x, i)).then_inc(x_in[par], 16)
                load(0, 0, True)
                sp.dma_start(wo[:, :, :], woT.rearrange("(k p) n -> p k n", p=P)).then_inc(w_in, 16)
                sp.dma_start(wg[:, :, :], gateT.rearrange("(k p) n -> p k n", p=P)).then_inc(w_in, 16)
                sp.dma_start(wn[:, :], w_norm).then_inc(w_in, 16)
                for k in range(CK):
                    sp.dma_start(we[:, k, :, :], expT[:, k * P:(k + 1) * P, :].rearrange("e p n -> p e n")).then_inc(w_in, 16)

                def step(i, par, nxt):
                    if nxt:
                        load(i + 1, 1 - par)
                    sp.wait_ge(r_ready, TT * (i + 1))
                    sp.dma_start(rows(x_out, i), res[:, :, :]).then_inc(stored, 16)
                phase_steps(sp, step)
                sp.wait_ge(stored, 16 * n_chunks)

            @block.gpsimd
            def _(pool):
                pool.wait_ge(ones, 2)
                nc.gpsimd.affine_select(out=lower[:, :, :, :], in_=lower[:, :, :, :], compare_op=ALU.is_gt, fill=0.0, base=0,
                                        pattern=[[0, TT], [1, NE], [-1, NE]], channel_multiplier=0).then_inc(masks, 1)
                nc.gpsimd.affine_select(out=upper[:, :, :, :], in_=upper[:, :, :, :], compare_op=ALU.is_ge, fill=0.0, base=0,
                                        pattern=[[0, TT], [-1, NE], [1, NE]], channel_multiplier=0).then_inc(masks, 1)

            @block.tensor
            def _(pe):
                pe.wait_ge(w_in, 80)

                def project(i):
                    pe.wait_ge(at_in, 32 * (i + 1))
                    pe.wait_ge(uT_sb, CK * i)
                    for t in range(TT):
                        for k in range(CK):
                            ins = nc.tensor.transpose(psum[:, BANK_A + k, t * P:(t + 1) * P],
                                                      aos[:, t, k * P:(k + 1) * P], ident[:, :])
                    ins.then_inc(aT_ps, 1)
                    pe.wait_ge(aT_sb, CK * (i + 1))
                    pe.wait_ge(l_sb, i)
                    for t in range(TT):
                        o = psum[:, BANK_O + t // 2, (t % 2) * C:(t % 2 + 1) * C]
                        for k in range(CK):
                            ins = nc.tensor.matmul(o, aT[:, k, t * P:(t + 1) * P], wo[:, k, :],
                                                   start=k == 0, stop=k == CK - 1)
                        if t % 2:
                            ins.then_inc(o_ps, 1)

                def gate(i, par):
                    for t in range(TT):
                        pe.wait_ge(u_ready, TT * i + t + 1)
                        for k in range(CK):
                            ins = nc.tensor.transpose(psum[:, BANK_A + k, t * P:(t + 1) * P],
                                                      un[:, t, k * P:(k + 1) * P], ident[:, :])
                    ins.then_inc(uT_ps, 1)
                    pe.wait_ge(uT_sb, CK * (i + 1))
                    for t in range(TT):
                        for k in range(CK):
                            ins = nc.tensor.matmul(psum[:, BANK_L, t * NE:(t + 1) * NE], uT[par][:, k, t * P:(t + 1) * P],
                                                   wg[:, k, :], start=k == 0, stop=k == CK - 1)
                    ins.then_inc(l_ps, 1)

                def experts(i, par, tiles):
                    for t in tiles:
                        for e in range(NP):
                            n = t * NP + e
                            pe.wait_ge(added, ADDED0 + TT * NE * i + 2 * (n - 3))
                            for k in range(CK):
                                ins = nc.tensor.matmul(psum[:, BANKS_E[n % 4], :], uT[par][:, k, t * P:(t + 1) * P],
                                                       we[:, k, 2 * e:2 * e + 2, :], start=k == 0, stop=k == CK - 1)
                            ins.then_inc(e_ps, 1)
                project(0)
                gate(0, 0)

                def step(i, par, nxt):
                    if nxt:
                        project(i + 1)
                    experts(i, par, range(0, TT - 1))
                    if nxt:
                        gate(i + 1, 1 - par)
                    experts(i, par, range(TT - 1, TT))
                phase_steps(pe, step)

            @block.scalar
            def _(act):
                act.wait_ge(w_in, 80)

                def first(i, par):
                    act.wait_ge(aT_ps, i + 1)
                    act.wait_ge(o_ps, 2 * i)
                    for k in range(CK):
                        nc.scalar.activation(aT[:, k, :], psum[:, BANK_A + k, :], ACT.Copy).then_inc(aT_sb, 1)
                    for t in range(TT):
                        act.wait_ge(h_ready, 2 * i + t // 2 + 1)
                        act.wait_ge(squares, TT * i + t)
                        if t == 0:
                            act.wait_ge(small, i)
                        nc.scalar.activation(sq[:, :], h[par][:, t, :], ACT.Square, accum_out=ss[:, t:t + 1]).then_inc(squares, 1)
                    act.wait_ge(inv_var, i + 1)
                    act.wait_ge(u_ready, TT * i)
                    nc.scalar.activation(rs[:, :], ri[:, :], ACT.Sqrt).then_inc(roots, 1)
                    act.wait_ge(uT_ps, i + 1)
                    if not (isinstance(i, int) and i < 2):
                        act.wait_ge(e_ps, TT * NP * (i - 1))
                    for k in range(CK):
                        nc.scalar.activation(uT[par][:, k, :], psum[:, BANK_A + k, :], ACT.Copy, scale=wn[:, k:k + 1]).then_inc(uT_sb, 1)
                    act.wait_ge(l_ps, i + 1)
                    act.wait_ge(gated, GATE * i + 3)
                    nc.scalar.activation(ex[:, :, :], dl[:, :, :], ACT.Exp).then_inc(exps, 1)

                first(0, 0)

                def step(i, par, nxt):
                    if nxt:
                        first(i + 1, 1 - par)
                phase_steps(act, step)

            @block.vector
            def _(dve):
                nc.vector.memset(lower[:, :, :, :], 1.0).then_inc(ones, 1)
                nc.vector.memset(upper[:, :, :, :], 1.0).then_inc(ones, 1)
                dve.wait_ge(masks, 2)

                def normalise(i, par):
                    for n in range(2):
                        dve.wait_ge(o_ps, 2 * i + n + 1)
                        dve.wait_ge(at_in, 32 * (i + 1))
                        nc.vector.tensor_tensor(h[par][:, 2 * n:2 * n + 2, :],
                                                psum[:, BANK_O + n, :].rearrange("p (t c) -> p t c", t=2),
                                                ts[:, 2 * n:2 * n + 2, :], ALU.add).then_inc(h_ready, 1)
                    dve.wait_ge(squares, TT * (i + 1))
                    nc.vector.tensor_scalar(va[:, :], ss[:, :], 1.0 / C, 1e-6, ALU.mult, ALU.add).then_inc(small, 1)
                    dve.wait_ge(small, i + 1)
                    nc.vector.reciprocal(ri[:, :], va[:, :]).then_inc(inv_var, 1)
                    dve.wait_ge(roots, i + 1)
                    dve.wait_ge(uT_ps, i)
                    for t in range(TT):
                        nc.vector.tensor_scalar(un[:, t, :], h[par][:, t, :], rs[:, t:t + 1], None, ALU.mult).then_inc(u_ready, 1)

                def choose(i, par):
                    done = [0]

                    def did(ins):
                        ins.then_inc(gated, 1)
                        done[0] += 1
                        dve.wait_ge(gated, GATE * i + done[0])
                    dve.wait_ge(l_ps, i + 1)
                    logits = psum[:, BANK_L, 0:TT * NE].rearrange("p (t e) -> p t e", t=TT)
                    nc.vector.tensor_copy(lg[:, :, :], logits).then_inc(l_sb, 1)
                    dve.wait_ge(l_sb, i + 1)
                    own = lg[:, :, :].unsqueeze(3).to_broadcast([P, TT, NE, NE])
                    other = lg[:, :, :].unsqueeze(2).to_broadcast([P, TT, NE, NE])
                    did(nc.vector.reduce_max(best[:, :], lg[:, :, :], AX.X))
                    did(nc.vector.tensor_copy(sel[:, :, :], best[:, :].unsqueeze(2).to_broadcast([P, TT, NE])))
                    did(nc.vector.tensor_tensor(dl[:, :, :], lg[:, :, :], sel[:, :, :], ALU.subtract))
                    did(nc.vector.tensor_tensor(gt[:, :, :, :], other, own, ALU.is_gt))
                    did(nc.vector.tensor_tensor(ge[:, :, :, :], other, own, ALU.is_ge))
                    did(nc.vector.tensor_tensor(gu[:, :, :, :], gt[:, :, :, :], upper[:, :, :, :], ALU.mult))
                    did(nc.vector.tensor_tensor(gl[:, :, :, :], ge[:, :, :, :], lower[:, :, :, :], ALU.mult))
                    did(nc.vector.tensor_tensor(above[:, :, :, :], gu[:, :, :, :], gl[:, :, :, :], ALU.add))
                    did(nc.vector.reduce_sum(rank[:, :, :], above[:, :, :, :], AX.X))
                    did(nc.vector.tensor_scalar(sel[:, :, :], rank[:, :, :], 1.5, None, ALU.is_lt))
                    dve.wait_ge(exps, i + 1)
                    did(nc.vector.tensor_tensor(lg[:, :, :], ex[:, :, :], sel[:, :, :], ALU.mult))
                    did(nc.vector.reduce_sum(den[:, :], lg[:, :, :], AX.X))
                    did(nc.vector.reciprocal(rden[:, :], den[:, :]))
                    if not (isinstance(i, int) and i < 2):
                        dve.wait_ge(added, ADDED0 + TT * NE * (i - 1))
                    nc.vector.tensor_tensor(comb[par][:, :, :], lg[:, :, :], rden[:, :].unsqueeze(2).to_broadcast([P, TT, NE]),
                                            ALU.mult).then_inc(comb_ready, 1)
                    assert done[0] == GATE

                def add_experts(i, par, tiles):
                    dve.wait_ge(comb_ready, i + 1)
                    for t in tiles:
                        for e in range(NE):
                            n = t * NE + e
                            if e % 2 == 0:
                                dve.wait_ge(e_ps, TT * NP * i + n // 2 + 1)
                            dve.wait_ge(added, ADDED0 + TT * NE * i + n)
                            so_far = h[par][:, t, :] if e == 0 else acc[:, (e - 1) % 2, :]
                            nc.vector.scalar_tensor_tensor(acc[:, e % 2, :], psum[:, BANKS_E[(n // 2) % 4], (e % 2) * C:(e % 2 + 1) * C],
                                                                 comb[par][:, t, e:e + 1], so_far, ALU.mult, ALU.add).then_inc(added, 1)
                        dve.wait_ge(added, ADDED0 + TT * NE * i + (t + 1) * NE)
                        if t == 0:
                            dve.wait_ge(x_in[par], 16 * (i // 2 + 1))
                            dve.wait_ge(stored, 16 * i)
                        nc.vector.scalar_tensor_tensor(res[:, t, :], acc[:, (NE - 1) % 2, :], 0.5, xs[par][:, t, :],
                                                       ALU.mult, ALU.add).then_inc(r_ready, 1)
                dve.sem_inc(added, ADDED0)
                normalise(0, 0)
                choose(0, 0)

                def step(i, par, nxt):
                    add_experts(i, par, range(0, 1))
                    if nxt:
                        normalise(i + 1, 1 - par)
                    add_experts(i, par, range(1, TT))
                    if nxt:
                        choose(i + 1, 1 - par)
                phase_steps(dve, step)


def mamba_in(nc, tag, psum, ident, x, base, xp, zs, w_norm, b_norm, inT, B, S):
    NC = S // CH
    n_chunks = B * NC
    with Phase(nc, tag) as ph:
        sb, sem = ph.sb, ph.sem
        xs = sb("xs", [P, TT, C])
        sn = sb("sn", [P, TT, C])
        an = sb("an", [P, TT, C])
        bs = sb("bs", [P, TT, C])
        aT = sb("aT", [P, CK, CH])
        xo, zo = sb("xo", [P, DM, CH]), sb("zo", [P, DM, CH])
        wn, bn = sb("wn", [P, CK]), sb("bn", [P, CK])
        wi = sb("wi", [P, CK, 2 * DI])
        zero = sb("zero", [P, DM, HALO])
        st6, mv = sb("st6", [P, TT, 6]), sb("mv", [P, TT, 2])
        va, vb, vc = (sb(n, [P, TT]) for n in ("va", "vb", "vc"))
        rq, rs = sb("rq", [P, 2, TT]), sb("rs", [P, 2, TT])
        w_in, x_in = sem("w_in"), sem("x_in")
        stats, small, inv_vars, roots = sem("stats"), sem("small"), sem("inv_vars"), sem("roots")
        dve_passed, sp_passed = sem("dve_passed"), sem("sp_passed")
        s_ready, a_ready, b_ready, b_stored = sem("s_ready"), sem("a_ready"), sem("b_ready"), sem("b_stored")
        aT_ps, aT_sb, x_ps, z_ps = sem("aT_ps"), sem("aT_sb"), sem("x_ps"), sem("z_ps")
        x_ready, z_ready, stored, zeroed = sem("x_ready"), sem("z_ready"), sem("stored"), sem("zeroed")

        with nc.Block() as block:
            @block.sync
            def _(sp):
                sp.dma_start(xs[:, :, :], rows(x, 0)).then_inc(x_in, 16)
                sp.dma_start(wn[:, :], w_norm).then_inc(w_in, 16)
                sp.dma_start(bn[:, :], b_norm).then_inc(w_in, 16)
                sp.dma_start(wi[:, :, :], inT.rearrange("(k p) n -> p k n", p=P)).then_inc(w_in, 16)
                sp.wait_ge(zeroed, 1)
                for b in range(B):
                    for at in (0, HALO + S):
                        sp.dma_start(xp[:, b, at:at + HALO].rearrange("(m p) t -> p m t", p=P), zero[:, :, :]).then_inc(zeroed, 16)

                def chunk(i, last):
                    if not last:
                        sp.wait_ge(b_ready, i + 1)
                        sp.dma_start(xs[:, :, :], rows(x, i + 1)).then_inc(x_in, 16)
                    sp.wait_ge(b_ready, i + 1)
                    sp.dma_start(rows(base, i), bs[:, :, :]).then_inc(b_stored, 16)
                    hold(sp, x_ready, DM * (i + 1), sp_passed)
                    sp.dma_start(xp[:, bass.ds(i // NC, 1), bass.ds((i % NC) * CH + HALO, CH)]
                                 .rearrange("(m p) o t -> p m (o t)", p=P), xo[:, :, :]).then_inc(stored, 16)
                    hold(sp, z_ready, DM * (i + 1), sp_passed)
                    sp.dma_start(cols(zs, i), zo[:, :, :]).then_inc(stored, 16)
                looped(sp, n_chunks, chunk)
                sp.wait_ge(b_stored, 16 * n_chunks)
                sp.wait_ge(stored, 32 * n_chunks)
                sp.wait_ge(zeroed, 1 + 32 * B)

            @block.vector
            def _(dve):
                nc.vector.memset(zero[:, :, :], 0.0).then_inc(zeroed, 1)

                def norm(i):
                    dve.wait_ge(x_in, 16 * (i + 1))
                    for t in range(TT):
                        nc.vector.bn_stats(st6[:, t, :], xs[:, t, :]).then_inc(stats, 1)
                    hold(dve, stats, 2 * TT * i + TT, dve_passed)
                    for t in range(TT):
                        nc.vector.bn_aggr(mv[:, t, :], st6[:, t, :]).then_inc(stats, 1)
                    dve.wait_ge(stats, 2 * TT * (i + 1))
                    nc.vector.tensor_scalar(va[:, :], mv[:, :, 1], 1e-5, None, ALU.add).then_inc(small, 1)
                    dve.wait_ge(small, 4 * i + 1)
                    nc.vector.reciprocal(rq[:, 0, :], va[:, :]).then_inc(small, 1)
                    dve.wait_ge(small, 4 * i + 2)
                    nc.vector.tensor_tensor(vb[:, :], mv[:, :, 1], rq[:, 0, :], ALU.mult).then_inc(small, 1)
                    dve.wait_ge(small, 4 * i + 3)
                    nc.vector.tensor_scalar(vc[:, :], vb[:, :], 1e-5, None, ALU.add).then_inc(small, 1)
                    dve.wait_ge(small, 4 * i + 4)
                    nc.vector.reciprocal(rq[:, 1, :], vc[:, :]).then_inc(inv_vars, 1)
                    dve.wait_ge(roots, i + 1)
                    for t in range(TT):
                        nc.vector.tensor_scalar(sn[:, t, :], xs[:, t, :], mv[:, t, 0:1], rs[:, 0, t:t + 1],
                                                ALU.subtract, ALU.mult).then_inc(s_ready, 1)
                    dve.wait_ge(aT_ps, i)
                    for t in range(TT):
                        dve.wait_ge(s_ready, TT * i + t + 1)
                        nc.vector.tensor_scalar(an[:, t, :], sn[:, t, :], rs[:, 1, t:t + 1], None,
                                                ALU.mult).then_inc(a_ready, 1)
                    dve.wait_ge(b_stored, 16 * i)
                    nc.vector.tensor_tensor(bs[:, :, :], xs[:, :, :], sn[:, :, :], ALU.add).then_inc(b_ready, 1)
                norm(0)

                def chunk(i, last):
                    if not last:
                        norm(i + 1)
                    dve.wait_ge(stored, 32 * i)
                    for m in range(DM):
                        dve.wait_ge(x_ps, DM * i + m + 1)
                        nc.vector.tensor_copy(xo[:, m, :], psum[:, 2 + m % 2, :]).then_inc(x_ready, 1)
                looped(dve, n_chunks, chunk)

            @block.tensor
            def _(pe):
                pe.wait_ge(w_in, 48)

                def chunk(i, last):
                    pe.wait_ge(aT_sb, CK * i)
                    for t in range(TT):
                        pe.wait_ge(a_ready, TT * i + t + 1)
                        for k in range(CK):
                            ins = nc.tensor.transpose(psum[:, k, t * P:(t + 1) * P], an[:, t, k * P:(k + 1) * P],
                                                      ident[:, :])
                    ins.then_inc(aT_ps, 1)
                    pe.wait_ge(aT_sb, CK * (i + 1))
                    for m in range(DM):
                        for half, bank, read, made in ((0, 2, x_ready, x_ps), (1, 4, z_ready, z_ps)):
                            if not (isinstance(i, int) and i == 0 and m < 2):
                                pe.wait_ge(read, DM * i + m - 1)
                            at = half * DI + m * P
                            for k in range(CK):
                                ins = nc.tensor.matmul(psum[:, bank + m % 2, :], wi[:, k, at:at + P], aT[:, k, :],
                                                       start=k == 0, stop=k == CK - 1)
                            ins.then_inc(made, 1)
                chunk(0, n_chunks == 1)
                if n_chunks > 2:
                    with pe.Fori(1, n_chunks - 1) as i:
                        chunk(i, False)
                if n_chunks > 1:
                    chunk(n_chunks - 1, True)

            @block.scalar
            def _(act):
                act.wait_ge(w_in, 48)

                def root(i):
                    act.wait_ge(inv_vars, i + 1)
                    act.wait_ge(a_ready, TT * i)
                    nc.scalar.activation(rs[:, :, :], rq[:, :, :], ACT.Sqrt).then_inc(roots, 1)

                def chunk(i, last):
                    act.wait_ge(aT_ps, i + 1)
                    act.wait_ge(z_ps, DM * i)
                    for k in range(CK):
                        nc.scalar.activation(aT[:, k, :], psum[:, k, :], ACT.Identity, scale=wn[:, k:k + 1],
                                             bias=bn[:, k:k + 1]).then_inc(aT_sb, 1)
                    if not last:
                        root(i + 1)
                    act.wait_ge(stored, 32 * i)
                    for m in range(DM):
                        act.wait_ge(z_ps, DM * i + m + 1)
                        nc.scalar.activation(zo[:, m, :], psum[:, 4 + m % 2, :], ACT.Silu).then_inc(z_ready, 1)
                root(0)
                looped(act, n_chunks, chunk)


def mamba_scan(nc, tag, psum, ident, reverse, xp, zs, y_other, y_out, conv_w, conv_b, xprojT, dtT, dt_b, a_log, d_w, B, S):
    NC = S // CH
    N = B * NC
    BC = 2 * DS
    flip = slice(None, None, -1) if reverse else slice(None)
    LAST = 0 if reverse else CH - 1
    HB, GB = 4, 3
    BANK_A, BANK_B, BANK_X = 4, 6, 7
    SLOT_X, SLOT_DT = 5, 8
    UNIT = [(n, m) for n in range(DS) for m in range(DM)]
    LOADS = 32 if reverse else 0

    with Phase(nc, tag) as ph:
        sb, sem = ph.sb, ph.sem
        win = sb("win", [P, DM, WIN])
        cv = sb("cv", [P, DM, CH])
        u = [sb(f"u{p}", [P, DM, CH]) for p in range(2)]
        dt = [sb(f"dt{p}", [P, DM, CH]) for p in range(2)]
        du = [sb(f"du{p}", [P, DM, CH]) for p in range(2)]
        sp1, sp2 = sb("sp1", [P, DM, CH]), sb("sp2", [P, DM, CH])
        bc = [sb(f"bc{p}", [3 * BC, CH], BF16) for p in range(2)]
        mid0 = sb("mid0", [BC, CH], BF16)
        rest = sb("rest", [BC, CH])
        xd = sb("xd", [BC + DTR, CH])
        sel = sb("sel", [3 * BC, BC, P], BF16)
        db = sb("db", [P, 3, CH])
        h = sb("h", [P, HB, CH])
        cs = sb("cs", [P, 2, CH])
        hc = sb("hc", [P, GB, CH])
        state = sb("state", [P, UNITS])
        yo = sb("yo", [P, DM, CH])
        if reverse:
            yt, yi, zi = sb("yt", [P, DM, CH]), sb("yi", [P, DM, CH]), sb("zi", [P, DM, CH])
        cw, cb, tb, dw = sb("cw", [P, DM, TAPS]), sb("cb", [P, DM]), sb("tb", [P, DM]), sb("dw", [P, DM])
        al, an = sb("al", [P, DM, DS]), sb("an", [P, DM, DS])
        wx = sb("wx", [P, DM, BC + DTR])
        wt = sb("wt", [BC + DTR, DI])
        sp_passed, dve_passed = sem("sp_passed"), sem("dve_passed")
        w_in, made, a_exp, a_neg = sem("w_in"), sem("made"), sem("a_exp"), sem("a_neg")
        win_in, tap0, taps, u_ready = sem("win_in"), sem("tap0"), sem("taps"), sem("u_ready")
        xp_ps, xd_sb, bc_high, bc_rest, bc_mid, bc_low = (sem(n) for n in ("xp_ps", "xd_sb", "bc_high", "bc_rest", "bc_mid", "bc_low"))
        dt_ps, dt_read, logs, dt_ready, du_ready = sem("dt_ps"), sem("dt_read"), sem("logs"), sem("dt_ready"), sem("du_ready")
        b_ps, c_ps, c_sb, decay, db_ready = sem("b_ps"), sem("c_ps"), sem("c_sb"), sem("decay"), sem("db_ready")
        scanned, carried, hc_ready, summed = sem("scanned"), sem("carried"), sem("hc_ready"), sem("summed")
        zeroed, y_read, y_mid, y_in, stored = sem("zeroed"), sem("y_read"), sem("y_mid"), sem("y_in"), sem("stored")
        y_ready = sem("y_ready") if reverse else y_read

        def place(i):
            return (2 * N - 1 - i) % N if reverse else i % N

        def in_steps(eng, step, start=None):
            with eng.Fori(0, B) as b:
                if start:
                    start(b)
                with eng.Fori(0, NC // 2) as c:
                    for par in range(2):
                        step(b * NC + c * 2 + par, par)

        with nc.Block() as block:
            @block.sync
            def _(sp):
                def load(i):
                    at = place(i)
                    sp.dma_start(win[:, :, :], xp[:, bass.ds(at // NC, 1), bass.ds((at % NC) * CH, WIN)]
                                 .rearrange("(m p) o t -> p m (o t)", p=P)).then_inc(win_in, 16)
                load(0)
                for dst, src in ((cw[:, :, :], conv_w), (cb[:, :], conv_b), (tb[:, :], dt_b), (dw[:, :], d_w), (al[:, :, :], a_log),
                                 (wx[:, :, :], xprojT.rearrange("(m p) n -> p m n", p=P)), (wt[BC:BC + DTR, :], dtT)):
                    sp.dma_start(dst, src).then_inc(w_in, 16)

                def step(i, par):
                    hold(sp, taps, DM * HALO * (i + 1), sp_passed)
                    load(i + 1)
                    if reverse:
                        hold(sp, y_ready, DM * i, sp_passed)
                        sp.dma_start(yi[:, :, :], cols(y_other, place(i))).then_inc(y_in, 16)
                        sp.dma_start(zi[:, :, :], cols(zs, place(i))).then_inc(y_in, 16)
                    hold(sp, y_ready, DM * (i + 1), sp_passed)
                    sp.dma_start(cols(y_out, place(i)), yo[:, :, :]).then_inc(stored, 16)
                in_steps(sp, step)
                sp.wait_ge(stored, 16 * N)
                sp.wait_ge(win_in, 16 * (N + 1))

            @block.gpsimd
            def _(pool):
                pool.wait_ge(made, 1)
                for part in range(3):
                    nc.gpsimd.affine_select(out=sel[:, :, :], in_=sel[:, :, :], compare_op=ALU.not_equal, fill=1.0,
                                            base=-part * BC, pattern=[[-1, BC], [0, P]], channel_multiplier=1).then_inc(made, 1)
                    pool.wait_ge(made, part + 2)

                def step(i, par):
                    for k, (n, m) in enumerate(UNIT):
                        pool.wait_ge(scanned, UNITS * i + k + 1)
                        if m == 0:
                            pool.wait_ge(c_sb, DS * i + n + 1)
                        if k >= GB:
                            pool.wait_ge(summed, UNITS * i + k - GB + 1)
                        elif k == 0:
                            pool.wait_ge(summed, UNITS * i)
                        nc.gpsimd.tensor_tensor(hc[:, k % GB, :], h[:, k % HB, :], cs[:, n % 2, :], ALU.mult).then_inc(hc_ready, 1)
                in_steps(pool, step)

            @block.tensor
            def _(pe):
                pe.wait_ge(w_in, 112)
                pe.wait_ge(made, 4)

                def x_proj(i, par):
                    pe.wait_ge(u_ready, DM * (i + 1))
                    for m in range(DM):
                        ins = nc.tensor.matmul(psum[0:BC + DTR, BANK_X, :], wx[:, m, :], u[par][:, m, :],
                                               start=m == 0, stop=m == DM - 1)
                    ins.then_inc(xp_ps, 1)
                    pe.wait_ge(xd_sb, i + 1)
                    pe.wait_ge(bc_high, i + 1)
                    pe.wait_ge(bc_rest, i + 1)

                def dt_proj(i, m):
                    nc.tensor.matmul(psum[:, BANK_X, :], wt[BC:BC + DTR, m * P:(m + 1) * P], xd[BC:BC + DTR, :],
                                     start=True, stop=True, tile_position=(BC, 0)).then_inc(dt_ps, 1)
                    pe.wait_ge(dt_read, 2 * (DM * i + m + 1))

                def sum_state(i, n):
                    for m in range(DM):
                        k = n * DM + m
                        pe.wait_ge(hc_ready, UNITS * i + k + 1)
                        nc.tensor.matmul(psum[:, m, :], ident[:, :], hc[:, k % GB, :], start=n == 0, stop=n == DS - 1
                                         ).then_inc(summed, 1)
                x_proj(0, 0)
                for m in range(DM):
                    dt_proj(0, m)

                def step(i, par):
                    pe.wait_ge(bc_mid, i + 1)
                    pe.wait_ge(bc_low, i + 1)
                    pe.wait_ge(y_read, DM * i)
                    for n in range(DS):
                        pe.wait_ge(c_sb, DS * i + n)
                        nc.tensor.matmul(psum[:, BANK_X, :], sel[:, DS + n, :], bc[par][:, :], start=True, stop=True).then_inc(c_ps, 1)
                        pe.wait_ge(db_ready, UNITS * i + n * DM)
                        nc.tensor.matmul(psum[:, BANK_B, :], sel[:, n, :], bc[par][:, :], start=True, stop=True).then_inc(b_ps, 1)
                        if n == SLOT_X:
                            pe.wait_ge(c_sb, DS * i + n + 1)
                            x_proj(i + 1, 1 - par)
                        if SLOT_DT <= n < SLOT_DT + DM:
                            pe.wait_ge(c_sb, DS * i + n + 1)
                            dt_proj(i + 1, n - SLOT_DT)
                        if n > 0:
                            sum_state(i, n - 1)
                    sum_state(i, DS - 1)
                in_steps(pe, step)

            @block.scalar
            def _(act):
                act.wait_ge(w_in, 112)
                nc.scalar.activation(an[:, :, :], al[:, :, :], ACT.Exp).then_inc(a_exp, 1)

                def prepare(i, par):
                    def first_tap(m):
                        act.wait_ge(win_in, 16 * (i + 1))
                        off = 2 * HALO if reverse else 0
                        nc.scalar.activation(cv[:, m, :], win[:, m, off:off + CH], ACT.Copy, scale=cw[:, m, 0:1]).then_inc(tap0, 1)

                    def silu(m):
                        act.wait_ge(taps, DM * HALO * i + DM * (HALO - 1) + m + 1)
                        nc.scalar.activation(u[par][:, m, :], cv[:, m, :], ACT.Silu, bias=cb[:, m:m + 1]).then_inc(u_ready, 1)

                    def split():
                        act.wait_ge(xp_ps, i + 1)
                        nc.scalar.activation(xd[BC:BC + DTR, :], psum[BC:BC + DTR, BANK_X, :], ACT.Copy).then_inc(xd_sb, 1)
                        nc.scalar.activation(bc[par][0:BC, :], psum[0:BC, BANK_X, :], ACT.Copy).then_inc(bc_high, 1)

                    def middle():
                        act.wait_ge(bc_rest, i + 1)
                        nc.scalar.activation(bc[par][BC:2 * BC, :], rest[:, :], ACT.Copy).then_inc(bc_mid, 1)

                    def softplus_in(m):
                        act.wait_ge(dt_ps, DM * i + m + 1)
                        act.wait_ge(dt_ready, DM * i)
                        nc.scalar.activation(sp1[:, m, :], psum[:, BANK_X, :], ACT.Abs, bias=tb[:, m:m + 1]).then_inc(dt_read, 1)
                        nc.scalar.activation(sp2[:, m, :], psum[:, BANK_X, :], ACT.Relu, bias=tb[:, m:m + 1]).then_inc(dt_read, 1)

                    def softplus_exp():
                        act.wait_ge(dt_read, 2 * DM * (i + 1))
                        nc.scalar.activation(sp1[:, :, :], sp1[:, :, :], ACT.Exp, scale=-1.0).then_inc(logs, 1)

                    def softplus_ln():
                        act.wait_ge(logs, 2 * i + 1)
                        nc.scalar.activation(sp1[:, :, :], sp1[:, :, :], ACT.Ln, bias=1.0).then_inc(logs, 1)
                    return ([(lambda m=m: first_tap(m)) for m in range(DM)], [(lambda m=m: silu(m)) for m in range(DM)], split, middle,
                            [(lambda m=m: softplus_in(m)) for m in range(DM)], softplus_exp, softplus_ln)

                taps_, silus, split, middle, ins_, exp_, ln_ = prepare(0, 0)
                for f in taps_ + silus + [split, middle] + ins_ + [exp_, ln_]:
                    f()
                act.wait_ge(a_neg, 1)

                def step(i, par):
                    taps_, silus, split, middle, ins_, exp_, ln_ = prepare(i + 1, 1 - par)
                    beside = {DM * SLOT_X + 1: [split], DM * SLOT_X + 3: [middle], DM * (SLOT_DT + DM) + 2: [exp_],
                              DM * (SLOT_DT + DM) + 4: [ln_], 14: silus}
                    for m in range(DM):
                        beside[m] = [taps_[m]]
                        beside[DM * (SLOT_DT + m) + 1] = [ins_[m]]
                    act.wait_ge(dt_ready, DM * (i + 1))

                    def carry(k):
                        act.wait_ge(scanned, UNITS * i + k + 1)
                        nc.scalar.activation(state[:, k:k + 1], h[:, k % HB, LAST:LAST + 1], ACT.Copy).then_inc(carried, 1)
                    for k, (n, m) in enumerate(UNIT):
                        if k >= 2:
                            act.wait_ge(scanned, UNITS * i + k - 1)
                        elif k == 0:
                            act.wait_ge(scanned, UNITS * i)
                        nc.scalar.activation(psum[:, BANK_A + k % 2, :], dt[par][:, m, :], ACT.Exp,
                                             scale=an[:, m, n:n + 1]).then_inc(decay, 1)
                        if m == 0:
                            act.wait_ge(c_ps, DS * i + n + 1)
                            if n > 1:
                                act.wait_ge(hc_ready, UNITS * i + DM * (n - 1))
                            elif n == 0:
                                act.wait_ge(hc_ready, UNITS * i)
                            nc.scalar.activation(cs[:, n % 2, :], psum[:, BANK_X, :], ACT.Copy).then_inc(c_sb, 1)
                        if k >= 2:
                            carry(k - 2)
                        for f in beside.get(k, ()):
                            f()
                    carry(UNITS - 2)
                    carry(UNITS - 1)
                in_steps(act, step)

            @block.vector
            def _(dve):
                nc.vector.memset(sel[:, :, :], 0.0).then_inc(made, 1)
                dve.wait_ge(a_exp, 1)
                nc.vector.tensor_scalar(an[:, :, :], an[:, :, :], -1.0, None, ALU.mult).then_inc(a_neg, 1)
                dve.wait_ge(w_in, 112)

                def prepare(i, par):
                    def tap(j, m):
                        done = DM * HALO * i + DM * (j - 1) + m
                        off = 2 * HALO - j if reverse else j
                        if j == 1:
                            dve.wait_ge(tap0, DM * i + m + 1)
                        else:
                            dve.wait_ge(taps, done - DM + 1)
                        nc.vector.scalar_tensor_tensor(cv[:, m, :], win[:, m, off:off + CH], cw[:, m, j:j + 1], cv[:, m, :],
                                                       ALU.mult, ALU.add).then_inc(taps, 1)

                    def split():
                        dve.wait_ge(bc_high, i + 1)
                        nc.vector.tensor_tensor(rest[:, :], psum[0:BC, BANK_X, :], bc[par][0:BC, :], ALU.subtract).then_inc(bc_rest, 1)
                        dve.wait_ge(bc_rest, i + 1)
                        nc.vector.tensor_copy(mid0[:, :], rest[:, :]).then_inc(made, 1)

                    def low():
                        dve.wait_ge(made, 4 + i + 1)
                        nc.vector.tensor_tensor(bc[par][2 * BC:3 * BC, :], rest[:, :], mid0[:, :], ALU.subtract).then_inc(bc_low, 1)

                    def softplus(m):
                        dve.wait_ge(logs, 2 * (i + 1))
                        nc.vector.tensor_tensor(dt[par][:, m, :], sp1[:, m, :], sp2[:, m, :], ALU.add).then_inc(dt_ready, 1)

                    def times_u(m):
                        dve.wait_ge(dt_ready, DM * i + m + 1)
                        nc.vector.tensor_tensor(du[par][:, m, :], dt[par][:, m, :], u[par][:, m, :], ALU.mult).then_inc(du_ready, 1)
                    return ([(lambda j=j, m=m: tap(j, m)) for j in range(1, TAPS) for m in range(DM)], split, low,
                            [(lambda m=m: softplus(m)) for m in range(DM)], [(lambda m=m: times_u(m)) for m in range(DM)])

                taps_, split, low, soft, times = prepare(0, 0)
                for f in taps_ + [split, low] + soft + times:
                    f()

                def start(b):
                    dve.wait_ge(carried, UNITS * NC * b)
                    nc.vector.memset(state[:, :], 0.0).then_inc(zeroed, 1)
                    hold(dve, zeroed, b + 1, dve_passed)

                def step(i, par):
                    taps_, split, low, soft, times = prepare(i + 1, 1 - par)
                    beside = {k + 1: [f] for k, f in enumerate(taps_)}
                    beside[DM * SLOT_X + 2] = [split]
                    beside[DM * SLOT_X + 4] = [low]
                    for m in range(DM):
                        beside[DM * (SLOT_DT + DM) + 6 + 2 * m] = [soft[m]]
                        beside[DM * (SLOT_DT + DM) + 7 + 2 * m] = [times[m]]

                    def times_b(k):
                        n, m = UNIT[k]
                        dve.wait_ge(b_ps, DS * i + n + 1)
                        if k < DM:
                            dve.wait_ge(du_ready, DM * (i + 1))
                        if k >= 3:
                            dve.wait_ge(scanned, UNITS * i + k - 2)
                        nc.vector.tensor_tensor(db[:, k % 3, :], du[par][:, m, :], psum[:, BANK_B, :], ALU.mult).then_inc(db_ready, 1)
                    times_b(0)
                    for k in range(UNITS):
                        if k + 1 < UNITS:
                            times_b(k + 1)
                        dve.wait_ge(decay, UNITS * i + k + 1)
                        dve.wait_ge(db_ready, UNITS * i + k + 1)
                        dve.wait_ge(carried, UNITS * i + max(0, k - HB + 1))
                        if k >= HB:
                            dve.wait_ge(hc_ready, UNITS * i + k - HB + 1)
                        elif k == 0:
                            dve.wait_ge(hc_ready, UNITS * i)
                        nc.vector.tensor_tensor_scan(h[:, k % HB, flip], psum[:, BANK_A + k % 2, flip], db[:, k % 3, flip],
                                                     state[:, k:k + 1], ALU.mult, ALU.add).then_inc(scanned, 1)
                        for f in beside.get(k, ()):
                            f()
                    for m in range(DM):
                        dve.wait_ge(summed, UNITS * i + UNITS - DM + m + 1)
                        dve.wait_ge(stored, 16 * i)
                        nc.vector.scalar_tensor_tensor((yt if reverse else yo)[:, m, :], u[par][:, m, :], dw[:, m:m + 1],
                                                       psum[:, m, :], ALU.mult, ALU.add).then_inc(y_read, 1)
                    if reverse:
                        dve.wait_ge(y_in, 32 * (i + 1))
                        for m in range(DM):
                            dve.wait_ge(y_read, DM * i + m + 1)
                            nc.vector.tensor_tensor(yt[:, m, :], yt[:, m, :], yi[:, m, :], ALU.add).then_inc(y_mid, 1)
                        for m in range(DM):
                            dve.wait_ge(y_mid, DM * i + m + 1)
                            nc.vector.tensor_tensor(yo[:, m, :], yt[:, m, :], zi[:, m, :], ALU.mult).then_inc(y_ready, 1)
                in_steps(dve, step, start)


def mamba_out(nc, tag, psum, y_in, base, x_out, outT, n_chunks):
    with Phase(nc, tag) as ph:
        sb, sem = ph.sb, ph.sem
        ys = [sb(f"ys{p}", [P, DM, CH]) for p in range(2)]
        bs = [sb(f"bs{p}", [P, TT, C]) for p in range(2)]
        res = sb("res", [P, TT, C])
        wo = sb("wo", [P, DM, C])
        w_in, loaded = sem("w_in"), [sem("loaded_even"), sem("loaded_odd")]
        o_ps, added, stored = sem("o_ps"), sem("added"), sem("stored")

        def phase_steps(eng, step):
            with eng.Fori(0, n_chunks // 2) as j:
                for par in range(2):
                    step(j * 2 + par, par)

        with nc.Block() as block:
            @block.sync
            def _(sp):
                def load(i, par, at):
                    sp.dma_start(ys[par][:, :, :], cols(y_in, at)).then_inc(loaded[par], 16)
                    sp.dma_start(bs[par][:, :, :], rows(base, at)).then_inc(loaded[par], 16)
                load(0, 0, 0)
                load(1, 1, 1)
                sp.dma_start(wo[:, :, :], outT.rearrange("(m p) n -> p m n", p=P)).then_inc(w_in, 16)

                def step(i, par):
                    sp.wait_ge(added, 2 * (i + 1))
                    sp.dma_start(rows(x_out, i), res[:, :, :]).then_inc(stored, 16)
                    load(i + 2, par, (i + 2) % n_chunks)
                phase_steps(sp, step)
                sp.wait_ge(stored, 16 * n_chunks)
                for par in range(2):
                    sp.wait_ge(loaded[par], 32 * (n_chunks // 2 + 1))

            @block.tensor
            def _(pe):
                pe.wait_ge(w_in, 16)

                def step(i, par):
                    pe.wait_ge(loaded[par], 32 * (i // 2 + 1))
                    pe.wait_ge(added, 2 * i)
                    for t in range(TT):
                        for m in range(DM):
                            ins = nc.tensor.matmul(psum[:, 2 * par + t // 2, (t % 2) * C:(t % 2 + 1) * C],
                                                   ys[par][:, m, t * P:(t + 1) * P], wo[:, m, :], start=m == 0, stop=m == DM - 1)
                        if t % 2:
                            ins.then_inc(o_ps, 1)
                phase_steps(pe, step)

            @block.vector
            def _(dve):
                def step(i, par):
                    dve.wait_ge(stored, 16 * i)
                    dve.wait_ge(loaded[par], 32 * (i // 2 + 1))
                    for n in range(2):
                        dve.wait_ge(o_ps, 2 * i + n + 1)
                        nc.vector.tensor_tensor(res[:, 2 * n:2 * n + 2, :],
                                                psum[:, 2 * par + n, :].rearrange("p (t c) -> p t c", t=2),
                                                bs[par][:, 2 * n:2 * n + 2, :], ALU.add).then_inc(added, 1)
                phase_steps(dve, step)


def macaron_block(nc, x, out, f, m, B, S):
    NT, N = B * S, B * S // CH
    scratch = lambda name, shape, dtype=F32: nc.dram_tensor(name, shape, dtype, kind="Internal").ap()
    t = scratch("t", (NT, C))
    qp = scratch("q_parts", (B * HEADS, 3, HD, S), BF16)
    kp = scratch("k_parts", (B * KVH, 3, HD, S), BF16)
    v = scratch("v", (B * KVH, S, HD))
    ao = scratch("ao", (NT, C))
    x1, x2 = scratch("x1", (NT, C)), scratch("x2", (NT, C))
    base = scratch("base", (NT, C))
    xp = scratch("xp", (DI, B, S + 2 * HALO))
    zs, y, yz = (scratch(n, (DI, NT)) for n in ("zs", "y", "yz"))
    with ExitStack() as ctx:
        psum = ctx.enter_context(nc.psum_tensor("psum", [P, 8, CH], F32))
        ident = ctx.enter_context(nc.sbuf_tensor("ident", [P, P], F32))

        def ffn(tag, x_in, x_out):
            ffn_in(nc, f"{tag}_in", psum, ident, x_in, t, qp, kp, v, f["norm1"], f["wqT"], f["wkT"], f["wvT"], B, S)
            attention(nc, f"{tag}_att", psum, ident, qp, kp, v, ao, B, S)
            ffn_out(nc, f"{tag}_out", psum, ident, ao, t, x_in, x_out, f["norm2"], f["woT"], f["gateT"], f["expT"], N)

        make_constants(nc, ident)
        ffn("ffn1", x, x1)
        mamba_in(nc, "mamba_in", psum, ident, x1, base, xp, zs, m["norm_w"], m["norm_b"], m["inT"], B, S)
        for tag, reverse, other, to in (("f", False, None, y), ("r", True, y, yz)):
            mamba_scan(nc, f"scan_{tag}", psum, ident, reverse, xp, zs, other, to, *(m[f"{n}_{tag}"] for n in
                       ("conv_w", "conv_b", "xprojT", "dtT", "dt_b", "a_log", "d")), B, S)
        mamba_out(nc, "mamba_out", psum, yz, base, x2, m["outT"], N)
        ffn("ffn2", x2, out)


def kernel(**inputs):
    import numpy as np
    import concourse.bacc as bacc
    from concourse.bass_utils import run_bass_kernel_spmd

    a = {k: np.asarray(v) for k, v in inputs.items()}
    B, S, _ = a["L0_attn_x"].shape
    turned = lambda w: np.ascontiguousarray(np.swapaxes(w, -1, -2))
    column = lambda w: np.ascontiguousarray(w.reshape(-1, P).T)
    tiles = lambda w: np.ascontiguousarray(w.reshape(-1, P, w.shape[-1]).swapaxes(0, 1))
    data = {"x": np.ascontiguousarray(a["L0_attn_x"].reshape(B * S, C))}
    ffn = {"norm1": column(a["L0_ffn_attn_norm_w"]), "norm2": column(a["L0_ffn_ffn_norm_w"]),
           "wqT": turned(a["L0_ffn_wq"]), "wkT": turned(a["L0_ffn_wk"]), "wvT": turned(a["L0_ffn_wv"]),
           "woT": turned(a["L0_ffn_wo"]), "gateT": turned(a["L0_ffn_gate_w"]), "expT": turned(a["L0_ffn_expert_w"])}
    mamba = {"norm_w": column(a["L0_attn_norm_w"]), "norm_b": column(a["L0_attn_norm_b"]),
             "inT": turned(a["L0_attn_in_proj_w"]), "outT": turned(a["L0_attn_out_proj_w"])}
    for d in "fr":
        xproj = a[f"L0_attn_x_proj_w_{d}"]
        mamba |= {
            f"conv_w_{d}": tiles(a[f"L0_attn_conv_w_{d}"].reshape(DI, TAPS)), f"conv_b_{d}": column(a[f"L0_attn_conv_b_{d}"]),
            f"xprojT_{d}": turned(np.concatenate([xproj[DTR:], xproj[:DTR]])),
            f"dtT_{d}": turned(a[f"L0_attn_dt_proj_w_{d}"]), f"dt_b_{d}": column(a[f"L0_attn_dt_proj_b_{d}"]),
            f"a_log_{d}": tiles(a[f"L0_attn_A_log_{d}"]), f"d_{d}": column(a[f"L0_attn_D_{d}"])}
    nc = bacc.Bacc("TRN2", target_bir_lowering=False, num_devices=1)
    aps = {}
    for part, arrays in (("", data), ("f_", ffn), ("m_", mamba)):
        aps[part] = {k: nc.dram_tensor(f"in_{part}{k}", w.shape, mybir.dt.from_np(w.dtype), kind="ExternalInput").ap()
                     for k, w in arrays.items()}
    out = nc.dram_tensor("out", (B * S, C), F32, kind="ExternalOutput").ap()
    macaron_block(nc, aps[""]["x"], out, aps["f_"], aps["m_"], B, S)
    given = {f"in_{part}{k}": w for part, arrays in (("", data), ("f_", ffn), ("m_", mamba)) for k, w in arrays.items()}
    r = run_bass_kernel_spmd(nc, [given], core_ids=[0])
    return r.results[0]["out"].reshape(B, S, C)
```

```python
import concourse.bass as bass
from concourse import mybir
from contextlib import ExitStack

F32 = mybir.dt.float32
BF16 = mybir.dt.bfloat16
ALU = mybir.AluOpType
ACT = mybir.ActivationFunctionType
AX = mybir.AxisListType

P = 128
C = 256
CK = C // P
CH = 512
TT = CH // P
HEADS, KVH, HD = 16, 4, 16
REP = HEADS // KVH
KW = KVH * HD
NE = 8
DI, DS, DTR = 512, 16, 16
DM = DI // P
TAPS = 4
HALO = TAPS - 1
WIN = CH + 2 * HALO
UNITS = DM * DS


class Phase:

    def __init__(self, nc, tag):
        self.nc, self.tag, self.ctx, self.sems = nc, tag, ExitStack(), []

    def __enter__(self):
        return self

    def sb(self, name, shape, dtype=F32):
        return self.ctx.enter_context(self.nc.sbuf_tensor(f"{self.tag}_{name}", shape, dtype))

    def sem(self, name):
        self.sems.append(self.nc.alloc_semaphore(f"{self.tag}_{name}"))
        return self.sems[-1]

    def __exit__(self, *exc):
        if exc[0] is None:
            self.nc.clear_and_free_semaphores(self.sems)
            self.nc.all_engine_barrier()
            self.ctx.close()
        return False


def looped(eng, n, body):
    if n > 1:
        with eng.Fori(0, n - 1) as i:
            body(i, False)
    body(n - 1, True)


def hold(eng, sem, value, passed):
    eng.wait_ge(sem, value)
    eng.sem_inc(passed, 1)


def rows(ap, i):
    return ap[bass.ds(i * CH, CH), :].rearrange("(t p) c -> p t c", p=P)


def cols(ap, i):
    return ap[:, bass.ds(i * CH, CH)].rearrange("(m p) t -> p m t", p=P)


def make_constants(nc, ident):
    with Phase(nc, "const") as ph:
        made = ph.sem("made")
        with nc.Block() as block:
            @block.gpsimd
            def _(pool):
                nc.gpsimd.memset(ident[:, :], 0.0).then_inc(made, 1)
                pool.wait_ge(made, 1)
                nc.gpsimd.affine_select(out=ident[:, :], in_=ident[:, :], compare_op=ALU.not_equal, fill=1.0,
                                        base=0, pattern=[[-1, P]], channel_multiplier=1).then_inc(made, 1)
                pool.wait_ge(made, 2)


def ffn_in(nc, tag, psum, ident, x, t_out, qp, kp, v_out, w_norm, wqT, wkT, wvT, B, S):
    NC = S // CH
    n_chunks = B * NC
    STORES = 16 * (TT + 3 * (CK + 1))
    with Phase(nc, tag) as ph:
        sb, sem = ph.sb, ph.sem
        xs = sb("xs", [P, TT, C])
        tn = sb("tn", [P, TT, C])
        an = sb("an", [P, TT, C])
        aT = sb("aT", [P, CK, CH])
        wn = sb("wn", [P, CK])
        wq = sb("wq", [P, CK, C])
        wk = sb("wk", [P, CK, KW])
        wv = sb("wv", [P, CK, KW])
        st6 = sb("st6", [P, TT, 6])
        mv = sb("mv", [P, TT, 2])
        va, vb, vc = (sb(n, [P, TT]) for n in ("va", "vb", "vc"))
        rq = sb("rq", [P, 2, TT])
        rs = sb("rs", [P, 2, TT])
        q3 = sb("q3", [P, 3, CK, CH], BF16)
        k3 = sb("k3", [KW, 3, CH], BF16)
        qr = sb("qr", [P, CK, CH])
        kr = sb("kr", [KW, CH])
        vs = sb("vs", [P, TT, KW])
        w_in, x_in = sem("w_in"), sem("x_in")
        stats, small, inv_vars, roots = sem("stats"), sem("small"), sem("inv_vars"), sem("roots")
        dve_passed, sp_passed = sem("dve_passed"), sem("sp_passed")
        t_ready, t_stored, a_ready = sem("t_ready"), sem("t_stored"), sem("a_ready")
        aT_ps, aT_sb, q_ps, k_ps, v_ps = sem("aT_ps"), sem("aT_sb"), sem("q_ps"), sem("k_ps"), sem("v_ps")
        high, rest, mid, low, v_ready = sem("high"), sem("rest"), sem("mid"), sem("low"), sem("v_ready")
        stored = sem("stored")

        with nc.Block() as block:
            @block.sync
            def _(sp):
                sp.dma_start(xs[:, :, :], rows(x, 0)).then_inc(x_in, 16)
                sp.dma_start(wq[:, :, :], wqT.rearrange("(k p) n -> p k n", p=P)).then_inc(w_in, 16)
                sp.dma_start(wk[:, :, :], wkT.rearrange("(k p) n -> p k n", p=P)).then_inc(w_in, 16)
                sp.dma_start(wv[:, :, :], wvT.rearrange("(k p) n -> p k n", p=P)).then_inc(w_in, 16)
                sp.dma_start(wn[:, :], w_norm).then_inc(w_in, 16)

                def chunk(i, last):
                    if not last:
                        sp.wait_ge(t_ready, TT * (i + 1))
                        sp.dma_start(xs[:, :, :], rows(x, i + 1)).then_inc(x_in, 16)
                    sp.wait_ge(t_ready, TT * (i + 1))
                    sp.dma_start(rows(t_out, i), tn[:, :, :]).then_inc(t_stored, 16)
                    sp.wait_ge(v_ready, i + 1)
                    b, token = i // NC, bass.ds((i % NC) * CH, CH)
                    for t in range(TT):
                        sp.dma_start(v_out[bass.ds(b * KVH, KVH), bass.ds((i % NC) * CH + t * P, P), :]
                                     .rearrange("g p d -> p g d"),
                                     vs[:, t, :].rearrange("p (g d) -> p g d", g=KVH)).then_inc(stored, 16)
                    for part, done in enumerate((high, mid, low)):
                        sp.wait_ge(done, 2 * (i + 1))
                        for m in range(CK):
                            heads = bass.ds(b * HEADS + m * (P // HD), P // HD)
                            sp.dma_start(qp[heads, part, :, token], q3[:, part, m, :]).then_inc(stored, 16)
                        sp.dma_start(kp[bass.ds(b * KVH, KVH), part, :, token], k3[:, part, :]).then_inc(stored, 16)
                looped(sp, n_chunks, chunk)
                sp.wait_ge(t_stored, 16 * n_chunks)
                sp.wait_ge(stored, STORES * n_chunks)

            @block.vector
            def _(dve):
                def norm(i):
                    dve.wait_ge(x_in, 16 * (i + 1))
                    for t in range(TT):
                        nc.vector.bn_stats(st6[:, t, :], xs[:, t, :]).then_inc(stats, 1)
                    hold(dve, stats, 2 * TT * i + TT, dve_passed)
                    for t in range(TT):
                        nc.vector.bn_aggr(mv[:, t, :], st6[:, t, :]).then_inc(stats, 1)
                    dve.wait_ge(stats, 2 * TT * (i + 1))
                    nc.vector.tensor_scalar(va[:, :], mv[:, :, 1], 1e-5, None, ALU.add).then_inc(small, 1)
                    dve.wait_ge(small, 4 * i + 1)
                    nc.vector.reciprocal(rq[:, 0, :], va[:, :]).then_inc(small, 1)
                    dve.wait_ge(small, 4 * i + 2)
                    nc.vector.tensor_tensor(vb[:, :], mv[:, :, 1], rq[:, 0, :], ALU.mult).then_inc(small, 1)
                    dve.wait_ge(small, 4 * i + 3)
                    nc.vector.tensor_scalar(vc[:, :], vb[:, :], 1e-6, None, ALU.add).then_inc(small, 1)
                    dve.wait_ge(small, 4 * i + 4)
                    nc.vector.reciprocal(rq[:, 1, :], vc[:, :]).then_inc(inv_vars, 1)
                    dve.wait_ge(roots, i + 1)
                    dve.wait_ge(t_stored, 16 * i)
                    for t in range(TT):
                        nc.vector.tensor_scalar(tn[:, t, :], xs[:, t, :], mv[:, t, 0:1], rs[:, 0, t:t + 1],
                                                ALU.subtract, ALU.mult).then_inc(t_ready, 1)
                    dve.wait_ge(aT_ps, i)
                    for t in range(TT):
                        dve.wait_ge(t_ready, TT * i + t + 1)
                        nc.vector.tensor_scalar(an[:, t, :], tn[:, t, :], rs[:, 1, t:t + 1], None,
                                                ALU.mult).then_inc(a_ready, 1)

                def split(i):
                    dve.wait_ge(q_ps, i + 1)
                    dve.wait_ge(high, 2 * i + 1)
                    nc.vector.tensor_tensor(qr[:, :, :], psum[:, 2:4, :], q3[:, 0, :, :], ALU.subtract).then_inc(rest, 1)
                    dve.wait_ge(high, 2 * i + 2)
                    nc.vector.tensor_tensor(kr[:, :], psum[0:KW, 4, :], k3[:, 0, :], ALU.subtract).then_inc(rest, 1)
                    dve.wait_ge(stored, STORES * i)
                    dve.wait_ge(mid, 2 * i + 1)
                    nc.vector.tensor_tensor(q3[:, 2, :, :], qr[:, :, :], q3[:, 1, :, :], ALU.subtract).then_inc(low, 1)
                    dve.wait_ge(mid, 2 * i + 2)
                    nc.vector.tensor_tensor(k3[:, 2, :], kr[:, :], k3[:, 1, :], ALU.subtract).then_inc(low, 1)

                norm(0)

                def chunk(i, last):
                    if not last:
                        norm(i + 1)
                    split(i)
                looped(dve, n_chunks, chunk)

            @block.tensor
            def _(pe):
                pe.wait_ge(w_in, 64)

                def chunk(i, last):
                    pe.wait_ge(aT_sb, CK * i)
                    for t in range(TT):
                        pe.wait_ge(a_ready, TT * i + t + 1)
                        for k in range(CK):
                            ins = nc.tensor.transpose(psum[:, k, t * P:(t + 1) * P], an[:, t, k * P:(k + 1) * P],
                                                      ident[:, :])
                    ins.then_inc(aT_ps, 1)
                    pe.wait_ge(aT_sb, CK * (i + 1))
                    pe.wait_ge(rest, 2 * i)
                    pe.wait_ge(v_ready, i)
                    for m in range(CK):
                        for k in range(CK):
                            ins = nc.tensor.matmul(psum[:, 2 + m, :], wq[:, k, m * P:(m + 1) * P], aT[:, k, :],
                                                   start=k == 0, stop=k == CK - 1)
                    ins.then_inc(q_ps, 1)
                    for k in range(CK):
                        ins = nc.tensor.matmul(psum[0:KW, 4, :], wk[:, k, :], aT[:, k, :],
                                               start=k == 0, stop=k == CK - 1)
                    ins.then_inc(k_ps, 1)
                    for t in range(TT):
                        for k in range(CK):
                            ins = nc.tensor.matmul(psum[:, 5, t * KW:(t + 1) * KW], aT[:, k, t * P:(t + 1) * P],
                                                   wv[:, k, :], start=k == 0, stop=k == CK - 1)
                    ins.then_inc(v_ps, 1)
                looped(pe, n_chunks, chunk)

            @block.scalar
            def _(act):
                act.wait_ge(w_in, 64)

                def root(i):
                    act.wait_ge(inv_vars, i + 1)
                    act.wait_ge(a_ready, TT * i)
                    nc.scalar.activation(rs[:, :, :], rq[:, :, :], ACT.Sqrt).then_inc(roots, 1)

                def chunk(i, last):
                    act.wait_ge(aT_ps, i + 1)
                    act.wait_ge(v_ps, i)
                    for k in range(CK):
                        nc.scalar.activation(aT[:, k, :], psum[:, k, :], ACT.Copy, scale=wn[:, k:k + 1]).then_inc(aT_sb, 1)
                    if not last:
                        root(i + 1)
                    act.wait_ge(q_ps, i + 1)
                    act.wait_ge(stored, STORES * i)
                    nc.scalar.activation(q3[:, 0, :, :], psum[:, 2:4, :], ACT.Copy).then_inc(high, 1)
                    act.wait_ge(k_ps, i + 1)
                    nc.scalar.activation(k3[:, 0, :], psum[0:KW, 4, :], ACT.Copy).then_inc(high, 1)
                    act.wait_ge(v_ps, i + 1)
                    nc.scalar.activation(vs[:, :, :], psum[:, 5, 0:TT * KW].rearrange("p (t n) -> p t n", n=KW),
                                         ACT.Copy).then_inc(v_ready, 1)
                    act.wait_ge(rest, 2 * i + 1)
                    nc.scalar.activation(q3[:, 1, :, :], qr[:, :, :], ACT.Copy).then_inc(mid, 1)
                    act.wait_ge(rest, 2 * i + 2)
                    nc.scalar.activation(k3[:, 1, :], kr[:, :], ACT.Copy).then_inc(mid, 1)
                root(0)
                looped(act, n_chunks, chunk)


PARTS = 6 * HD
SROWS = PARTS + 3
VW = 32
NEG = -3.0e38


def attention(nc, tag, psum, ident, qp, kp, v_in, ao, B, S):
    NT_Q = S // P
    NQB = S // CH
    N = B * KVH
    MROWS = REP * NT_Q
    blocks = [(qb, kb) for qb in range(NQB) for kb in range(TT * (qb + 1))]
    pieces = [(i, h, c) for i in range(NT_Q) for h in range(REP) for c in range(0, i + 1, TT)]
    NB, NP = len(blocks), len(pieces)
    M_START, M_END = NB // 8, NB - max(2, NB // 10)
    M_TURN = M_END + 1
    before = [NP * (min(max(s, M_START), M_END) - M_START) // (M_END - M_START) for s in range(NB + 1)]
    share = [pieces[before[s]:before[s + 1]] for s in range(NB)]
    PB = 4
    LAG = 2
    E0, PV0 = 1, PB - 1

    def closes(s):
        return s >= 0 and blocks[s][1] == TT * (blocks[s][0] + 1) - 1

    uses = []
    for s in range(NB):
        uses += [("piece", n) for n in range(before[s], before[s + 1])]
        uses += [("out", blocks[s - LAG - 1][0])] * closes(s - LAG - 1) + [("max", 0)] * (s == M_TURN)
    uses += [("out", NQB - 1)]
    place = {use: n for n, use in enumerate(uses)}
    turn_bank = lambda use: 5 + place[use] % 3
    last_use = lambda use: uses[place[use] - 3] if place[use] >= 3 else None

    def last_piece(n):
        return max((j for j in range(n) if turn_bank(("piece", j)) == turn_bank(("piece", n))), default=-1)

    def diag(s):
        qb, kb = blocks[s]
        return kb - TT * qb

    with Phase(nc, tag) as ph:
        sb, sem = ph.sb, ph.sem
        Q = [sb(f"q{p}", [SROWS, REP, S], BF16) for p in range(2)]
        K = [sb(f"k{p}", [SROWS, S], BF16) for p in range(2)]
        V = [sb(f"v{p}", [P, S // P, VW]) for p in range(2)]
        E = sb("e", [P, PB, REP, CH])
        O = sb("o", [P, CH])
        on = sb("on", [P, TT, REP, HD])
        rec = sb("rec", [P, TT, REP])
        mask = sb("mask", [P, P], BF16)
        identb = sb("identb", [P, P], BF16)
        mx = sb("mx", [P, MROWS, NQB])
        nm = sb("nm", [P, MROWS])
        m3 = sb("m3", [MROWS, 3, P], BF16)
        mr = sb("mr", [MROWS, P])
        made, loaded = sem("made"), [sem("loaded_even"), sem("loaded_odd")]
        m_ps, m_red, n_max, mT_ps = sem("m_ps"), sem("m_red"), sem("n_max"), sem("mT_ps")
        m_high, m_rest, m_mid, m_low, m_in = sem("m_high"), sem("m_rest"), sem("m_mid"), sem("m_low"), sem("m_in")
        sp_passed, pool_passed, pe_passed = sem("sp_passed"), sem("pool_passed"), sem("pe_passed")
        s_ps, e_ready, masked, pv = sem("s_ps"), sem("e_ready"), sem("masked"), sem("pv")
        o_sb, oT_ps, recip, normed, stored = sem("o_sb"), sem("oT_ps"), sem("recip"), sem("normed"), sem("stored")
        BANK_O = 4

        def phase_steps(eng, step):
            if N > 2:
                with eng.Fori(0, N // 2 - 1) as j:
                    step(j * 2, 0, True, True)
                    step(j * 2 + 1, 1, True, True)
            step(N - 2, 0, True, False)
            step(N - 1, 1, False, False)

        with nc.Block() as block:
            @block.sync
            def _(sp):
                def load(it, par):
                    b, g = it // KVH, it % KVH
                    q, k, v = Q[par], K[par], V[par]
                    row = 0
                    for n in (3, 2, 1):
                        src = qp[bass.ds(it * REP, REP), 0:n, :, :]
                        sp.dma_start(q[row:row + n * HD, :, :], src.rearrange("h p d t -> (p d) h t")).then_inc(loaded[par], 16)
                        for r in range(n):
                            sp.dma_start(k[row + r * HD:row + (r + 1) * HD, :],
                                         kp[bass.ds(it, 1), 3 - n, :, :].rearrange("o d t -> (o d) t")).then_inc(loaded[par], 16)
                        row += n * HD
                    sp.dma_start(v[:, :, 0:HD], v_in[bass.ds(it, 1), :, :].rearrange("o (n p) d -> p (o n) d", p=P)
                                 ).then_inc(loaded[par], 16)

                def put_maxima(it, par):
                    for p_ in range(3):
                        sp.wait_ge((m_high, m_mid, m_low)[p_], it + 1)
                        sp.dma_start(Q[par][PARTS + p_:PARTS + p_ + 1, :, :], m3[:, p_, :]).then_inc(m_in, 16)

                sp.wait_ge(made, 9)
                load(0, 0)
                load(1, 1)
                put_maxima(0, 0)

                def step(it, par, nxt, ld):
                    b, g = it // KVH, it % KVH
                    for qb in range(NQB):
                        if nxt and qb == NQB - 1:
                            put_maxima(it + 1, 1 - par)
                        sp.wait_ge(normed, it * NQB + qb + 1)
                        sp.dma_start(ao[bass.ds(b * S + qb * CH, CH), bass.ds(g * REP * HD, REP * HD)]
                                     .rearrange("(t p) c -> p t c", p=P),
                                     on[:, :, :, :].rearrange("p t h d -> p t (h d)")).then_inc(stored, 16)
                    if ld:
                        hold(sp, pv, PV0 + (it + 1) * NB, sp_passed)
                        load(it + 2, par)
                phase_steps(sp, step)
                sp.wait_ge(stored, 16 * NQB * N)

            @block.gpsimd
            def _(pool):
                pool.wait_ge(made, 8)
                nc.gpsimd.affine_select(out=mask[:, :], in_=mask[:, :], compare_op=ALU.is_ge, fill=NEG, base=0,
                                        pattern=[[-1, P]], channel_multiplier=1).then_inc(made, 1)

                def step(it, par, nxt, ld):
                    for s in range(NB):
                        if diag(s) >= 0:
                            off = diag(s) * P
                            hold(pool, e_ready, E0 + 2 * (it * NB + s + 1), pool_passed)
                            part = E[:, s % PB, :, off:off + P]
                            nc.gpsimd.affine_select(out=part, in_=part, compare_op=ALU.is_ge, fill=0.0, base=0,
                                                    pattern=[[0, REP], [1, P]], channel_multiplier=-1).then_inc(masked, 1)
                phase_steps(pool, step)

            @block.tensor
            def _(pe):
                pe.sem_inc(pv, PV0)
                pe.wait_ge(made, 9)

                def bank_is_free(it, use):
                    kind, n = last_use(use) or ("none", 0)
                    if kind == "piece":
                        pe.wait_ge(m_red, (it + 1) * NP + n + 1)
                    elif kind == "out":
                        pe.wait_ge(normed, it * NQB + n + 1)
                    elif kind == "max":
                        pe.wait_ge(m_high, it + 2)
                        pe.wait_ge(m_rest, it + 2)
                    elif kind == "none":
                        pe.wait_ge(m_red, (it + 1) * NP)
                        pe.wait_ge(m_rest, it + 1)
                        pe.wait_ge(normed, it * NQB)

                def maxima(it, par, first, todo, beside=True):
                    q, k = Q[par], K[par]
                    if first == 0 and todo:
                        pe.wait_ge(loaded[par], 160 * (it // 2 + 1))
                    for n, (i, h, c) in enumerate(todo, first):
                        if not beside:
                            if last_piece(n) >= 0:
                                pe.wait_ge(m_red, last_piece(n) + 1)
                        else:
                            bank_is_free(it - 1, ("piece", n))
                        w = min(TT, i + 1 - c) * P
                        bank = psum[:, turn_bank(("piece", n)), :]
                        is_diag = c + TT > i
                        ins = nc.tensor.matmul(bank[:, 0:w], q[0:PARTS, h, i * P:(i + 1) * P], k[0:PARTS, c * P:c * P + w],
                                               start=True, stop=not is_diag)
                        if is_diag:
                            ins = nc.tensor.matmul(bank[:, w - P:w], identb[:, :], mask[:, :], start=False, stop=True)
                        ins.then_inc(m_ps, 1)

                def turn_maxima(it):
                    hold(pe, n_max, it + 1, pe_passed)
                    nc.tensor.transpose(psum[0:MROWS, turn_bank(("max", 0)), 0:P], nm[:, :], ident[:, :]).then_inc(mT_ps, 1)

                def weighted(it, par, s, half):
                    qb, kb = blocks[s]
                    off = max(diag(s), 0) * P
                    lo, hi = max(off, half * CH // 2), (half + 1) * CH // 2
                    if half == 0:
                        pe.wait_ge(e_ready, E0 + 2 * (it * NB + s + 1))
                        if diag(s) >= 0:
                            n_diag = sum(diag(z) >= 0 for z in range(s + 1))
                            pe.wait_ge(masked, it * NQB * TT + n_diag)
                        if kb == 0:
                            pe.wait_ge(o_sb, it * NQB + qb)
                    if lo < hi:
                        for h in range(REP):
                            ins = nc.tensor.matmul(psum[32 * h:32 * h + VW, BANK_O, lo:hi], V[par][:, kb, :],
                                                   E[:, s % PB, h, lo:hi], start=kb == 0 and half == 0, stop=closes(s) and half == 1,
                                                   tile_position=(0, 32 * h))
                        if half:
                            ins.then_inc(pv, 1)

                def turn_output(it, qb, nxt):
                    pe.wait_ge(o_sb, it * NQB + qb + 1)
                    if nxt:
                        bank_is_free(it, ("out", qb))
                    else:
                        pe.wait_ge(normed, it * NQB + qb)
                    for t in range(TT):
                        ins = nc.tensor.transpose(psum[:, turn_bank(("out", qb)), t * P:(t + 1) * P], O[:, t * P:(t + 1) * P], ident[:, :])
                    ins.then_inc(oT_ps, 1)

                for s in range(NB):
                    maxima(0, 0, before[s], share[s], beside=False)
                turn_maxima(0)

                def step(it, par, nxt, ld):
                    q, k = Q[par], K[par]
                    pe.wait_ge(m_in, 48 * (it + 1))
                    for s in range(NB):
                        qb, kb = blocks[s]
                        off = max(diag(s), 0) * P

                        def score(h):
                            if h % 2 == 0:
                                pe.wait_ge(e_ready, E0 + 2 * (it * NB + s) + h // 2 - 1)
                            ins = nc.tensor.matmul(psum[:, h, off:CH], k[:, kb * P:(kb + 1) * P],
                                                   q[:, h, qb * CH + off:(qb + 1) * CH], start=True, stop=True)
                            if h % 2:
                                ins.then_inc(s_ps, 1)

                        made_m, n_m, span = 0, len(share[s]) if nxt else 0, 2 * REP

                        def maxima_up_to(at):
                            upto = min(n_m, -(-at * n_m // span))
                            maxima(it + 1, 1 - par, before[s] + made_m, share[s][made_m:upto])
                            return max(upto, made_m)
                        for h in range(REP):
                            made_m = maxima_up_to(h + 1 if h == 0 else h)
                            score(h)
                        for half in range(2):
                            made_m = maxima_up_to(REP + 2 * half)
                            if s >= LAG:
                                weighted(it, par, s - LAG, half)
                        made_m = maxima_up_to(span)
                        if closes(s - LAG - 1):
                            turn_output(it, blocks[s - LAG - 1][0], nxt)
                        if nxt and s == M_TURN:
                            bank_is_free(it, ("max", 0))
                            turn_maxima(it + 1)
                    for s in range(NB - LAG, NB):
                        weighted(it, par, s, 0)
                        weighted(it, par, s, 1)
                    turn_output(it, NQB - 1, nxt)
                phase_steps(pe, step)

            @block.scalar
            def _(act):
                def split_high(it):
                    act.wait_ge(mT_ps, it + 1)
                    act.wait_ge(m_in, 48 * it)
                    nc.scalar.activation(m3[:, 0, :], psum[0:MROWS, turn_bank(("max", 0)), 0:P], ACT.Copy).then_inc(m_high, 1)

                def split_middle(it):
                    act.wait_ge(m_rest, it + 1)
                    nc.scalar.activation(m3[:, 1, :], mr[:, :], ACT.Copy).then_inc(m_mid, 1)

                act.sem_inc(e_ready, E0)
                split_high(0)
                split_middle(0)

                def step(it, par, nxt, ld):
                    for s in range(NB):
                        off = max(diag(s), 0) * P
                        for hp in range(2):
                            act.wait_ge(s_ps, 2 * (it * NB + s) + hp + 1)
                            if hp == 0:
                                act.wait_ge(pv, PV0 + it * NB + s - PB + 1)
                            nc.scalar.activation(E[:, s % PB, 2 * hp:2 * hp + 2, off:CH], psum[:, 2 * hp:2 * hp + 2, off:CH],
                                                 ACT.Exp, scale=HD ** -0.5).then_inc(e_ready, 1)
                        if closes(s - LAG):
                            output(it, s - LAG)
                        if nxt and s == M_TURN:
                            split_high(it + 1)
                            split_middle(it + 1)
                    output(it, NB - 1)

                def output(it, s):
                    qb = blocks[s][0]
                    act.wait_ge(pv, PV0 + it * NB + s + 1)
                    act.wait_ge(oT_ps, it * NQB + qb)
                    nc.scalar.activation(O[:, :], psum[:, BANK_O, :], ACT.Copy).then_inc(o_sb, 1)
                phase_steps(act, step)

            @block.vector
            def _(dve):
                for p in range(2):
                    nc.vector.memset(V[p][:, :, HD:VW], 0.0).then_inc(made, 1)
                    nc.vector.memset(K[p][PARTS:SROWS, :], 1.0).then_inc(made, 1)
                dve.wait_ge(made, 4)
                for p in range(2):
                    nc.vector.memset(V[p][:, :, HD:HD + 1], 1.0).then_inc(made, 1)
                nc.vector.memset(mask[:, :], 0.0).then_inc(made, 1)
                nc.vector.tensor_copy(identb[:, :], ident[:, :]).then_inc(made, 1)
                nc.vector.memset(mx[:, :, :], NEG).then_inc(recip, 1)

                def reduce(it, first, todo):
                    for n, (i, h, c) in enumerate(todo, first):
                        dve.wait_ge(m_ps, it * NP + n + 1)
                        if n == 0:
                            dve.wait_ge(n_max, it)
                        w = min(TT, i + 1 - c) * P
                        nc.vector.reduce_max(mx[:, h * NT_Q + i, c // TT:c // TT + 1], psum[:, turn_bank(("piece", n)), 0:w],
                                             AX.X).then_inc(m_red, 1)

                def negate(it):
                    dve.wait_ge(m_red, (it + 1) * NP)
                    dve.wait_ge(mT_ps, it)
                    nc.vector.tensor_reduce(nm[:, :], mx[:, :, :], AX.X, ALU.max, negate=True).then_inc(n_max, 1)

                def split(it):
                    dve.wait_ge(m_high, it + 1)
                    nc.vector.tensor_tensor(mr[:, :], psum[0:MROWS, turn_bank(("max", 0)), 0:P], m3[:, 0, :], ALU.subtract).then_inc(m_rest, 1)
                    dve.wait_ge(m_mid, it + 1)
                    nc.vector.tensor_tensor(m3[:, 2, :], mr[:, :], m3[:, 1, :], ALU.subtract).then_inc(m_low, 1)

                def normalise(it, qb):
                    dve.wait_ge(oT_ps, it * NQB + qb + 1)
                    o = psum[:, turn_bank(("out", qb)), :].rearrange("p (t h d) -> p t h d", t=TT, h=REP)
                    dve.wait_ge(normed, it * NQB + qb)
                    nc.vector.reciprocal(rec[:, :, :], o[:, :, :, HD]).then_inc(recip, 1)
                    dve.wait_ge(recip, it * NQB + qb + 2)
                    dve.wait_ge(stored, 16 * (it * NQB + qb))
                    nc.vector.tensor_tensor(on[:, :, :, :], o[:, :, :, 0:HD],
                                            rec[:, :, :].unsqueeze(3).to_broadcast([P, TT, REP, HD]), ALU.mult
                                            ).then_inc(normed, 1)
                dve.wait_ge(recip, 1)
                for s in range(NB):
                    reduce(0, before[s], share[s])
                negate(0)
                split(0)

                def step(it, par, nxt, ld):
                    for s in range(NB):
                        if nxt:
                            reduce(it + 1, before[s], share[s])
                        if closes(s - LAG - 1):
                            normalise(it, blocks[s - LAG - 1][0])
                        if nxt and s == M_END - 1:
                            negate(it + 1)
                    if nxt:
                        split(it + 1)
                    normalise(it, NQB - 1)
                phase_steps(dve, step)


def ffn_out(nc, tag, psum, ident, ao, t_in, x, x_out, w_norm, woT, gateT, expT, n_chunks):
    NP = NE // 2
    GATE = 13
    ADDED0 = 6
    with Phase(nc, tag) as ph:
        sb, sem = ph.sb, ph.sem
        aos = sb("aos", [P, TT, C])
        ts = sb("ts", [P, TT, C])
        xs = [sb(f"xs{p}", [P, TT, C]) for p in range(2)]
        h = [sb(f"h{p}", [P, TT, C]) for p in range(2)]
        un = sb("un", [P, TT, C])
        aT = sb("aT", [P, CK, CH])
        uT = [sb(f"uT{p}", [P, CK, CH]) for p in range(2)]
        acc = sb("acc", [P, 2, C])
        res = sb("res", [P, TT, C])
        sq = sb("sq", [P, C])
        ss, va, ri, rs = (sb(n, [P, TT]) for n in ("ss", "va", "ri", "rs"))
        lg, ex, sel = (sb(n, [P, TT, NE]) for n in ("lg", "ex", "sel"))
        comb = [sb(f"comb{p}", [P, TT, NE]) for p in range(2)]
        gt, ge, gl, gu, above = (sb(n, [P, TT, NE, NE]) for n in ("gt", "ge", "gl", "gu", "above"))
        best, rank, den, rden = sb("best", [P, TT]), sb("rank", [P, TT, NE]), sb("den", [P, TT]), sb("rden", [P, TT])
        dl = sb("dl", [P, TT, NE])
        lower = sb("lower", [P, TT, NE, NE])
        upper = sb("upper", [P, TT, NE, NE])
        wn = sb("wn", [P, CK])
        wo = sb("wo", [P, CK, C])
        wg = sb("wg", [P, CK, NE])
        we = sb("we", [P, CK, NE, C])
        w_in, ones, masks, sp_passed = sem("w_in"), sem("ones"), sem("masks"), sem("sp_passed")
        at_in, x_in = sem("at_in"), [sem("x_in_even"), sem("x_in_odd")]
        aT_ps, aT_sb, o_ps, h_ready = sem("aT_ps"), sem("aT_sb"), sem("o_ps"), sem("h_ready")
        squares, inv_var, roots, small = sem("squares"), sem("inv_var"), sem("roots"), sem("small")
        u_ready, uT_ps, uT_sb, l_ps = sem("u_ready"), sem("uT_ps"), sem("uT_sb"), sem("l_ps")
        l_sb, gated, exps, comb_ready = sem("l_sb"), sem("gated"), sem("exps"), sem("comb_ready")
        e_ps, added, r_ready, stored = sem("e_ps"), sem("added"), sem("r_ready"), sem("stored")
        BANK_A, BANK_O, BANK_L, BANKS_E = 0, 2, 2, (4, 5, 6, 7)

        def phase_steps(eng, step):
            if n_chunks > 2:
                with eng.Fori(0, n_chunks // 2 - 1) as j:
                    step(j * 2, 0, True)
                    step(j * 2 + 1, 1, True)
            step(n_chunks - 2, 0, True)
            step(n_chunks - 1, 1, False)

        with nc.Block() as block:
            @block.sync
            def _(sp):
                def load(i, par, first=False):
                    if not first:
                        hold(sp, aT_ps, i, sp_passed)
                        hold(sp, h_ready, 2 * i, sp_passed)
                    sp.dma_start(aos[:, :, :], rows(ao, i)).then_inc(at_in, 16)
                    sp.dma_start(ts[:, :, :], rows(t_in, i)).then_inc(at_in, 16)
                    if not first:
                        sp.wait_ge(r_ready, TT * (i - 1))
                    sp.dma_start(xs[par][:, :, :], rows(x, i)).then_inc(x_in[par], 16)
                load(0, 0, True)
                sp.dma_start(wo[:, :, :], woT.rearrange("(k p) n -> p k n", p=P)).then_inc(w_in, 16)
                sp.dma_start(wg[:, :, :], gateT.rearrange("(k p) n -> p k n", p=P)).then_inc(w_in, 16)
                sp.dma_start(wn[:, :], w_norm).then_inc(w_in, 16)
                for k in range(CK):
                    sp.dma_start(we[:, k, :, :], expT[:, k * P:(k + 1) * P, :].rearrange("e p n -> p e n")).then_inc(w_in, 16)

                def step(i, par, nxt):
                    if nxt:
                        load(i + 1, 1 - par)
                    sp.wait_ge(r_ready, TT * (i + 1))
                    sp.dma_start(rows(x_out, i), res[:, :, :]).then_inc(stored, 16)
                phase_steps(sp, step)
                sp.wait_ge(stored, 16 * n_chunks)

            @block.gpsimd
            def _(pool):
                pool.wait_ge(ones, 2)
                nc.gpsimd.affine_select(out=lower[:, :, :, :], in_=lower[:, :, :, :], compare_op=ALU.is_gt, fill=0.0, base=0,
                                        pattern=[[0, TT], [1, NE], [-1, NE]], channel_multiplier=0).then_inc(masks, 1)
                nc.gpsimd.affine_select(out=upper[:, :, :, :], in_=upper[:, :, :, :], compare_op=ALU.is_ge, fill=0.0, base=0,
                                        pattern=[[0, TT], [-1, NE], [1, NE]], channel_multiplier=0).then_inc(masks, 1)

            @block.tensor
            def _(pe):
                pe.wait_ge(w_in, 80)

                def project(i):
                    pe.wait_ge(at_in, 32 * (i + 1))
                    pe.wait_ge(uT_sb, CK * i)
                    for t in range(TT):
                        for k in range(CK):
                            ins = nc.tensor.transpose(psum[:, BANK_A + k, t * P:(t + 1) * P],
                                                      aos[:, t, k * P:(k + 1) * P], ident[:, :])
                    ins.then_inc(aT_ps, 1)
                    pe.wait_ge(aT_sb, CK * (i + 1))
                    pe.wait_ge(l_sb, i)
                    for t in range(TT):
                        o = psum[:, BANK_O + t // 2, (t % 2) * C:(t % 2 + 1) * C]
                        for k in range(CK):
                            ins = nc.tensor.matmul(o, aT[:, k, t * P:(t + 1) * P], wo[:, k, :],
                                                   start=k == 0, stop=k == CK - 1)
                        if t % 2:
                            ins.then_inc(o_ps, 1)

                def gate(i, par):
                    for t in range(TT):
                        pe.wait_ge(u_ready, TT * i + t + 1)
                        for k in range(CK):
                            ins = nc.tensor.transpose(psum[:, BANK_A + k, t * P:(t + 1) * P],
                                                      un[:, t, k * P:(k + 1) * P], ident[:, :])
                    ins.then_inc(uT_ps, 1)
                    pe.wait_ge(uT_sb, CK * (i + 1))
                    for t in range(TT):
                        for k in range(CK):
                            ins = nc.tensor.matmul(psum[:, BANK_L, t * NE:(t + 1) * NE], uT[par][:, k, t * P:(t + 1) * P],
                                                   wg[:, k, :], start=k == 0, stop=k == CK - 1)
                    ins.then_inc(l_ps, 1)

                def experts(i, par, tiles):
                    for t in tiles:
                        for e in range(NP):
                            n = t * NP + e
                            pe.wait_ge(added, ADDED0 + TT * NE * i + 2 * (n - 3))
                            for k in range(CK):
                                ins = nc.tensor.matmul(psum[:, BANKS_E[n % 4], :], uT[par][:, k, t * P:(t + 1) * P],
                                                       we[:, k, 2 * e:2 * e + 2, :], start=k == 0, stop=k == CK - 1)
                            ins.then_inc(e_ps, 1)
                project(0)
                gate(0, 0)

                def step(i, par, nxt):
                    if nxt:
                        project(i + 1)
                    experts(i, par, range(0, TT - 1))
                    if nxt:
                        gate(i + 1, 1 - par)
                    experts(i, par, range(TT - 1, TT))
                phase_steps(pe, step)

            @block.scalar
            def _(act):
                act.wait_ge(w_in, 80)

                def first(i, par):
                    act.wait_ge(aT_ps, i + 1)
                    act.wait_ge(o_ps, 2 * i)
                    for k in range(CK):
                        nc.scalar.activation(aT[:, k, :], psum[:, BANK_A + k, :], ACT.Copy).then_inc(aT_sb, 1)
                    for t in range(TT):
                        act.wait_ge(h_ready, 2 * i + t // 2 + 1)
                        act.wait_ge(squares, TT * i + t)
                        if t == 0:
                            act.wait_ge(small, i)
                        nc.scalar.activation(sq[:, :], h[par][:, t, :], ACT.Square, accum_out=ss[:, t:t + 1]).then_inc(squares, 1)
                    act.wait_ge(inv_var, i + 1)
                    act.wait_ge(u_ready, TT * i)
                    nc.scalar.activation(rs[:, :], ri[:, :], ACT.Sqrt).then_inc(roots, 1)
                    act.wait_ge(uT_ps, i + 1)
                    if not (isinstance(i, int) and i < 2):
                        act.wait_ge(e_ps, TT * NP * (i - 1))
                    for k in range(CK):
                        nc.scalar.activation(uT[par][:, k, :], psum[:, BANK_A + k, :], ACT.Copy, scale=wn[:, k:k + 1]).then_inc(uT_sb, 1)
                    act.wait_ge(l_ps, i + 1)
                    act.wait_ge(gated, GATE * i + 3)
                    nc.scalar.activation(ex[:, :, :], dl[:, :, :], ACT.Exp).then_inc(exps, 1)

                first(0, 0)

                def step(i, par, nxt):
                    if nxt:
                        first(i + 1, 1 - par)
                phase_steps(act, step)

            @block.vector
            def _(dve):
                nc.vector.memset(lower[:, :, :, :], 1.0).then_inc(ones, 1)
                nc.vector.memset(upper[:, :, :, :], 1.0).then_inc(ones, 1)
                dve.wait_ge(masks, 2)

                def normalise(i, par):
                    for n in range(2):
                        dve.wait_ge(o_ps, 2 * i + n + 1)
                        dve.wait_ge(at_in, 32 * (i + 1))
                        nc.vector.tensor_tensor(h[par][:, 2 * n:2 * n + 2, :],
                                                psum[:, BANK_O + n, :].rearrange("p (t c) -> p t c", t=2),
                                                ts[:, 2 * n:2 * n + 2, :], ALU.add).then_inc(h_ready, 1)
                    dve.wait_ge(squares, TT * (i + 1))
                    nc.vector.tensor_scalar(va[:, :], ss[:, :], 1.0 / C, 1e-6, ALU.mult, ALU.add).then_inc(small, 1)
                    dve.wait_ge(small, i + 1)
                    nc.vector.reciprocal(ri[:, :], va[:, :]).then_inc(inv_var, 1)
                    dve.wait_ge(roots, i + 1)
                    dve.wait_ge(uT_ps, i)
                    for t in range(TT):
                        nc.vector.tensor_scalar(un[:, t, :], h[par][:, t, :], rs[:, t:t + 1], None, ALU.mult).then_inc(u_ready, 1)

                def choose(i, par):
                    done = [0]

                    def did(ins):
                        ins.then_inc(gated, 1)
                        done[0] += 1
                        dve.wait_ge(gated, GATE * i + done[0])
                    dve.wait_ge(l_ps, i + 1)
                    logits = psum[:, BANK_L, 0:TT * NE].rearrange("p (t e) -> p t e", t=TT)
                    nc.vector.tensor_copy(lg[:, :, :], logits).then_inc(l_sb, 1)
                    dve.wait_ge(l_sb, i + 1)
                    own = lg[:, :, :].unsqueeze(3).to_broadcast([P, TT, NE, NE])
                    other = lg[:, :, :].unsqueeze(2).to_broadcast([P, TT, NE, NE])
                    did(nc.vector.reduce_max(best[:, :], lg[:, :, :], AX.X))
                    did(nc.vector.tensor_copy(sel[:, :, :], best[:, :].unsqueeze(2).to_broadcast([P, TT, NE])))
                    did(nc.vector.tensor_tensor(dl[:, :, :], lg[:, :, :], sel[:, :, :], ALU.subtract))
                    did(nc.vector.tensor_tensor(gt[:, :, :, :], other, own, ALU.is_gt))
                    did(nc.vector.tensor_tensor(ge[:, :, :, :], other, own, ALU.is_ge))
                    did(nc.vector.tensor_tensor(gu[:, :, :, :], gt[:, :, :, :], upper[:, :, :, :], ALU.mult))
                    did(nc.vector.tensor_tensor(gl[:, :, :, :], ge[:, :, :, :], lower[:, :, :, :], ALU.mult))
                    did(nc.vector.tensor_tensor(above[:, :, :, :], gu[:, :, :, :], gl[:, :, :, :], ALU.add))
                    did(nc.vector.reduce_sum(rank[:, :, :], above[:, :, :, :], AX.X))
                    did(nc.vector.tensor_scalar(sel[:, :, :], rank[:, :, :], 1.5, None, ALU.is_lt))
                    dve.wait_ge(exps, i + 1)
                    did(nc.vector.tensor_tensor(lg[:, :, :], ex[:, :, :], sel[:, :, :], ALU.mult))
                    did(nc.vector.reduce_sum(den[:, :], lg[:, :, :], AX.X))
                    did(nc.vector.reciprocal(rden[:, :], den[:, :]))
                    if not (isinstance(i, int) and i < 2):
                        dve.wait_ge(added, ADDED0 + TT * NE * (i - 1))
                    nc.vector.tensor_tensor(comb[par][:, :, :], lg[:, :, :], rden[:, :].unsqueeze(2).to_broadcast([P, TT, NE]),
                                            ALU.mult).then_inc(comb_ready, 1)
                    assert done[0] == GATE

                def add_experts(i, par, tiles):
                    dve.wait_ge(comb_ready, i + 1)
                    for t in tiles:
                        for e in range(NE):
                            n = t * NE + e
                            if e % 2 == 0:
                                dve.wait_ge(e_ps, TT * NP * i + n // 2 + 1)
                            dve.wait_ge(added, ADDED0 + TT * NE * i + n)
                            so_far = h[par][:, t, :] if e == 0 else acc[:, (e - 1) % 2, :]
                            nc.vector.scalar_tensor_tensor(acc[:, e % 2, :], psum[:, BANKS_E[(n // 2) % 4], (e % 2) * C:(e % 2 + 1) * C],
                                                                 comb[par][:, t, e:e + 1], so_far, ALU.mult, ALU.add).then_inc(added, 1)
                        dve.wait_ge(added, ADDED0 + TT * NE * i + (t + 1) * NE)
                        if t == 0:
                            dve.wait_ge(x_in[par], 16 * (i // 2 + 1))
                            dve.wait_ge(stored, 16 * i)
                        nc.vector.scalar_tensor_tensor(res[:, t, :], acc[:, (NE - 1) % 2, :], 0.5, xs[par][:, t, :],
                                                       ALU.mult, ALU.add).then_inc(r_ready, 1)
                dve.sem_inc(added, ADDED0)
                normalise(0, 0)
                choose(0, 0)

                def step(i, par, nxt):
                    add_experts(i, par, range(0, 1))
                    if nxt:
                        normalise(i + 1, 1 - par)
                    add_experts(i, par, range(1, TT))
                    if nxt:
                        choose(i + 1, 1 - par)
                phase_steps(dve, step)


def mamba_in(nc, tag, psum, ident, x, base, xp, zs, w_norm, b_norm, inT, B, S):
    NC = S // CH
    n_chunks = B * NC
    with Phase(nc, tag) as ph:
        sb, sem = ph.sb, ph.sem
        xs = sb("xs", [P, TT, C])
        sn = sb("sn", [P, TT, C])
        an = sb("an", [P, TT, C])
        bs = sb("bs", [P, TT, C])
        aT = sb("aT", [P, CK, CH])
        xo, zo = sb("xo", [P, DM, CH]), sb("zo", [P, DM, CH])
        wn, bn = sb("wn", [P, CK]), sb("bn", [P, CK])
        wi = sb("wi", [P, CK, 2 * DI])
        zero = sb("zero", [P, DM, HALO])
        st6, mv = sb("st6", [P, TT, 6]), sb("mv", [P, TT, 2])
        va, vb, vc = (sb(n, [P, TT]) for n in ("va", "vb", "vc"))
        rq, rs = sb("rq", [P, 2, TT]), sb("rs", [P, 2, TT])
        w_in, x_in = sem("w_in"), sem("x_in")
        stats, small, inv_vars, roots = sem("stats"), sem("small"), sem("inv_vars"), sem("roots")
        dve_passed, sp_passed = sem("dve_passed"), sem("sp_passed")
        s_ready, a_ready, b_ready, b_stored = sem("s_ready"), sem("a_ready"), sem("b_ready"), sem("b_stored")
        aT_ps, aT_sb, x_ps, z_ps = sem("aT_ps"), sem("aT_sb"), sem("x_ps"), sem("z_ps")
        x_ready, z_ready, stored, zeroed = sem("x_ready"), sem("z_ready"), sem("stored"), sem("zeroed")

        with nc.Block() as block:
            @block.sync
            def _(sp):
                sp.dma_start(xs[:, :, :], rows(x, 0)).then_inc(x_in, 16)
                sp.dma_start(wn[:, :], w_norm).then_inc(w_in, 16)
                sp.dma_start(bn[:, :], b_norm).then_inc(w_in, 16)
                sp.dma_start(wi[:, :, :], inT.rearrange("(k p) n -> p k n", p=P)).then_inc(w_in, 16)
                sp.wait_ge(zeroed, 1)
                for b in range(B):
                    for at in (0, HALO + S):
                        sp.dma_start(xp[:, b, at:at + HALO].rearrange("(m p) t -> p m t", p=P), zero[:, :, :]).then_inc(zeroed, 16)

                def chunk(i, last):
                    if not last:
                        sp.wait_ge(b_ready, i + 1)
                        sp.dma_start(xs[:, :, :], rows(x, i + 1)).then_inc(x_in, 16)
                    sp.wait_ge(b_ready, i + 1)
                    sp.dma_start(rows(base, i), bs[:, :, :]).then_inc(b_stored, 16)
                    hold(sp, x_ready, DM * (i + 1), sp_passed)
                    sp.dma_start(xp[:, bass.ds(i // NC, 1), bass.ds((i % NC) * CH + HALO, CH)]
                                 .rearrange("(m p) o t -> p m (o t)", p=P), xo[:, :, :]).then_inc(stored, 16)
                    hold(sp, z_ready, DM * (i + 1), sp_passed)
                    sp.dma_start(cols(zs, i), zo[:, :, :]).then_inc(stored, 16)
                looped(sp, n_chunks, chunk)
                sp.wait_ge(b_stored, 16 * n_chunks)
                sp.wait_ge(stored, 32 * n_chunks)
                sp.wait_ge(zeroed, 1 + 32 * B)

            @block.vector
            def _(dve):
                nc.vector.memset(zero[:, :, :], 0.0).then_inc(zeroed, 1)

                def norm(i):
                    dve.wait_ge(x_in, 16 * (i + 1))
                    for t in range(TT):
                        nc.vector.bn_stats(st6[:, t, :], xs[:, t, :]).then_inc(stats, 1)
                    hold(dve, stats, 2 * TT * i + TT, dve_passed)
                    for t in range(TT):
                        nc.vector.bn_aggr(mv[:, t, :], st6[:, t, :]).then_inc(stats, 1)
                    dve.wait_ge(stats, 2 * TT * (i + 1))
                    nc.vector.tensor_scalar(va[:, :], mv[:, :, 1], 1e-5, None, ALU.add).then_inc(small, 1)
                    dve.wait_ge(small, 4 * i + 1)
                    nc.vector.reciprocal(rq[:, 0, :], va[:, :]).then_inc(small, 1)
                    dve.wait_ge(small, 4 * i + 2)
                    nc.vector.tensor_tensor(vb[:, :], mv[:, :, 1], rq[:, 0, :], ALU.mult).then_inc(small, 1)
                    dve.wait_ge(small, 4 * i + 3)
                    nc.vector.tensor_scalar(vc[:, :], vb[:, :], 1e-5, None, ALU.add).then_inc(small, 1)
                    dve.wait_ge(small, 4 * i + 4)
                    nc.vector.reciprocal(rq[:, 1, :], vc[:, :]).then_inc(inv_vars, 1)
                    dve.wait_ge(roots, i + 1)
                    for t in range(TT):
                        nc.vector.tensor_scalar(sn[:, t, :], xs[:, t, :], mv[:, t, 0:1], rs[:, 0, t:t + 1],
                                                ALU.subtract, ALU.mult).then_inc(s_ready, 1)
                    dve.wait_ge(aT_ps, i)
                    for t in range(TT):
                        dve.wait_ge(s_ready, TT * i + t + 1)
                        nc.vector.tensor_scalar(an[:, t, :], sn[:, t, :], rs[:, 1, t:t + 1], None,
                                                ALU.mult).then_inc(a_ready, 1)
                    dve.wait_ge(b_stored, 16 * i)
                    nc.vector.tensor_tensor(bs[:, :, :], xs[:, :, :], sn[:, :, :], ALU.add).then_inc(b_ready, 1)
                norm(0)

                def chunk(i, last):
                    if not last:
                        norm(i + 1)
                    dve.wait_ge(stored, 32 * i)
                    for m in range(DM):
                        dve.wait_ge(x_ps, DM * i + m + 1)
                        nc.vector.tensor_copy(xo[:, m, :], psum[:, 2 + m % 2, :]).then_inc(x_ready, 1)
                looped(dve, n_chunks, chunk)

            @block.tensor
            def _(pe):
                pe.wait_ge(w_in, 48)

                def chunk(i, last):
                    pe.wait_ge(aT_sb, CK * i)
                    for t in range(TT):
                        pe.wait_ge(a_ready, TT * i + t + 1)
                        for k in range(CK):
                            ins = nc.tensor.transpose(psum[:, k, t * P:(t + 1) * P], an[:, t, k * P:(k + 1) * P],
                                                      ident[:, :])
                    ins.then_inc(aT_ps, 1)
                    pe.wait_ge(aT_sb, CK * (i + 1))
                    for m in range(DM):
                        for half, bank, read, made in ((0, 2, x_ready, x_ps), (1, 4, z_ready, z_ps)):
                            if not (isinstance(i, int) and i == 0 and m < 2):
                                pe.wait_ge(read, DM * i + m - 1)
                            at = half * DI + m * P
                            for k in range(CK):
                                ins = nc.tensor.matmul(psum[:, bank + m % 2, :], wi[:, k, at:at + P], aT[:, k, :],
                                                       start=k == 0, stop=k == CK - 1)
                            ins.then_inc(made, 1)
                chunk(0, n_chunks == 1)
                if n_chunks > 2:
                    with pe.Fori(1, n_chunks - 1) as i:
                        chunk(i, False)
                if n_chunks > 1:
                    chunk(n_chunks - 1, True)

            @block.scalar
            def _(act):
                act.wait_ge(w_in, 48)

                def root(i):
                    act.wait_ge(inv_vars, i + 1)
                    act.wait_ge(a_ready, TT * i)
                    nc.scalar.activation(rs[:, :, :], rq[:, :, :], ACT.Sqrt).then_inc(roots, 1)

                def chunk(i, last):
                    act.wait_ge(aT_ps, i + 1)
                    act.wait_ge(z_ps, DM * i)
                    for k in range(CK):
                        nc.scalar.activation(aT[:, k, :], psum[:, k, :], ACT.Identity, scale=wn[:, k:k + 1],
                                             bias=bn[:, k:k + 1]).then_inc(aT_sb, 1)
                    if not last:
                        root(i + 1)
                    act.wait_ge(stored, 32 * i)
                    for m in range(DM):
                        act.wait_ge(z_ps, DM * i + m + 1)
                        nc.scalar.activation(zo[:, m, :], psum[:, 4 + m % 2, :], ACT.Silu).then_inc(z_ready, 1)
                root(0)
                looped(act, n_chunks, chunk)


def mamba_scan(nc, tag, psum, ident, reverse, xp, zs, y_other, y_out, conv_w, conv_b, xprojT, dtT, dt_b, a_log, d_w, B, S):
    NC = S // CH
    N = B * NC
    BC = 2 * DS
    flip = slice(None, None, -1) if reverse else slice(None)
    LAST = 0 if reverse else CH - 1
    DB, HB, GB, CB = 8, 8, 8, 4
    BANK_A = 4
    bank = lambda n: 6 + n % 2
    SLOT_X, SLOT_DT = 4, 5
    K_Y, K_TAPS, K_SILU, K_EXP, K_LN, K_SOFT, K_DU = 4, 6, 8, 38, 42, 47, 50
    LOOKAHEAD = 5
    HC0, SUM0, CAR0 = (CB - 1) * DM, GB, HB
    assert UNITS % DB == UNITS % HB == UNITS % GB == DS % CB == 0
    GROUP = 4 if NC % 4 == 0 else 2
    UNIT = [(n, m) for n in range(DS) for m in range(DM)]

    with Phase(nc, tag) as ph:
        sb, sem = ph.sb, ph.sem
        win = sb("win", [P, DM, WIN])
        cv = sb("cv", [P, DM, CH])
        u = [sb(f"u{p}", [P, DM, CH]) for p in range(2)]
        dt = [sb(f"dt{p}", [P, DM, CH]) for p in range(2)]
        du = [sb(f"du{p}", [P, DM, CH]) for p in range(2)]
        sp1, sp2 = sb("sp1", [P, DM, CH]), sb("sp2", [P, DM, CH])
        bc = [sb(f"bc{p}", [3 * BC, CH], BF16) for p in range(2)]
        mid0 = sb("mid0", [BC, CH], BF16)
        rest = sb("rest", [BC, CH])
        xd = sb("xd", [BC + DTR, CH])
        sel = sb("sel", [3 * BC, BC, P], BF16)
        db = sb("db", [P, DB, CH])
        h = sb("h", [P, HB, CH])
        cs = sb("cs", [P, CB, CH])
        hc = sb("hc", [P, GB, CH])
        state = sb("state", [P, UNITS])
        yo = sb("yo", [P, DM, CH])
        if reverse:
            yt, yi, zi = sb("yt", [P, DM, CH]), sb("yi", [P, DM, CH]), sb("zi", [P, DM, CH])
        cw, cb, tb, dw = sb("cw", [P, DM, TAPS]), sb("cb", [P, DM]), sb("tb", [P, DM]), sb("dw", [P, DM])
        al, an = sb("al", [P, DM, DS]), sb("an", [P, DM, DS])
        wx = sb("wx", [P, DM, BC + DTR])
        wt = sb("wt", [BC + DTR, DI])
        sp_passed, dve_passed = sem("sp_passed"), sem("dve_passed")
        w_in, made, a_exp, a_neg = sem("w_in"), sem("made"), sem("a_exp"), sem("a_neg")
        win_in, tap0, taps, u_ready = sem("win_in"), sem("tap0"), sem("taps"), sem("u_ready")
        xp_ps, xd_sb, bc_high, bc_rest, bc_mid, bc_low = (sem(n) for n in ("xp_ps", "xd_sb", "bc_high", "bc_rest", "bc_mid", "bc_low"))
        dt_ps, dt_read, logs, dt_ready, du_ready = sem("dt_ps"), sem("dt_read"), sem("logs"), sem("dt_ready"), sem("du_ready")
        b_ps, c_ps, c_sb, decay, db_ready = sem("b_ps"), sem("c_ps"), sem("c_sb"), sem("decay"), sem("db_ready")
        scanned, carried, hc_ready, summed = sem("scanned"), sem("carried"), sem("hc_ready"), sem("summed")
        zeroed, y_read, stored = sem("zeroed"), sem("y_read"), sem("stored")
        y_in, z_in, y_added = sem("y_in"), sem("z_in"), sem("y_added")
        y_ready = sem("y_ready") if reverse else y_read

        def place(i):
            return (2 * N - 1 - i) % N if reverse else i % N

        def in_steps(eng, step, start=None):
            with eng.Fori(0, B) as b:
                if start:
                    start(b)
                with eng.Fori(0, NC // GROUP) as c:
                    for r in range(GROUP):
                        step(b * NC + c * GROUP + r, r % 2, r > 0, r < GROUP - 1)

        with nc.Block() as block:
            @block.sync
            def _(sp):
                def load(i):
                    at = place(i)
                    sp.dma_start(win[:, :, :], xp[:, bass.ds(at // NC, 1), bass.ds((at % NC) * CH, WIN)]
                                 .rearrange("(m p) o t -> p m (o t)", p=P)).then_inc(win_in, 16)
                def store(i):
                    hold(sp, y_ready, DM * (i + 1), sp_passed)
                    sp.dma_start(cols(y_out, place(i)), yo[:, :, :]).then_inc(stored, 16)
                load(0)
                if reverse:
                    sp.dma_start(yi[:, :, :], cols(y_other, place(0))).then_inc(y_in, 16)
                for dst, src in ((cw[:, :, :], conv_w), (cb[:, :], conv_b), (tb[:, :], dt_b), (dw[:, :], d_w), (al[:, :, :], a_log),
                                 (wx[:, :, :], xprojT.rearrange("(m p) n -> p m n", p=P)), (wt[BC:BC + DTR, :], dtT)):
                    sp.dma_start(dst, src).then_inc(w_in, 16)

                def step(i, par, pending, put_off):
                    hold(sp, taps, DM * HALO * (i + 1), sp_passed)
                    load(i + 1)
                    if pending:
                        store(i - 1)
                    if reverse:
                        hold(sp, y_ready, DM * i, sp_passed)
                        sp.dma_start(zi[:, :, :], cols(zs, place(i))).then_inc(z_in, 16)
                        hold(sp, y_added, DM * (i + 1), sp_passed)
                        sp.dma_start(yi[:, :, :], cols(y_other, place(i + 1))).then_inc(y_in, 16)
                    if not put_off:
                        store(i)
                in_steps(sp, step)
                sp.wait_ge(stored, 16 * N)
                sp.wait_ge(win_in, 16 * (N + 1))
                if reverse:
                    sp.wait_ge(y_in, 16 * (N + 1))

            @block.gpsimd
            def _(pool):
                pool.wait_ge(made, 1)
                for part in range(3):
                    nc.gpsimd.affine_select(out=sel[:, :, :], in_=sel[:, :, :], compare_op=ALU.not_equal, fill=1.0,
                                            base=-part * BC, pattern=[[-1, BC], [0, P]], channel_multiplier=1).then_inc(made, 1)
                    pool.wait_ge(made, part + 2)

                pool.sem_inc(hc_ready, HC0)

                def times_u(i, par, m):
                    pool.wait_ge(dt_ready, DM * i + m + 1)
                    nc.gpsimd.tensor_tensor(du[par][:, m, :], dt[par][:, m, :], u[par][:, m, :], ALU.mult).then_inc(du_ready, 1)
                for m in range(DM):
                    times_u(0, 0, m)

                def step(i, par, pending, put_off):
                    for k, (n, m) in enumerate(UNIT):
                        pool.wait_ge(scanned, UNITS * i + k + 1)
                        if m == 0:
                            pool.wait_ge(c_sb, DS * i + n + 1)
                        pool.wait_ge(summed, SUM0 + UNITS * i + k - GB + 1)
                        nc.gpsimd.tensor_tensor(hc[:, k % GB, :], h[:, k % HB, :], cs[:, n % CB, :], ALU.mult).then_inc(hc_ready, 1)
                        if K_DU <= k < K_DU + 2 * DM and (k - K_DU) % 2 == 0:
                            times_u(i + 1, 1 - par, (k - K_DU) // 2)
                in_steps(pool, step)

            @block.tensor
            def _(pe):
                pe.wait_ge(w_in, 112)
                pe.wait_ge(made, 4)

                pe.sem_inc(summed, SUM0)

                def x_proj(i, par, at):
                    pe.wait_ge(u_ready, DM * (i + 1))
                    for m in range(DM):
                        ins = nc.tensor.matmul(psum[0:BC + DTR, at, :], wx[:, m, :], u[par][:, m, :],
                                               start=m == 0, stop=m == DM - 1)
                    ins.then_inc(xp_ps, 1)

                def dt_proj(i, m, at):
                    pe.wait_ge(xd_sb, i + 1)
                    nc.tensor.matmul(psum[:, at, :], wt[BC:BC + DTR, m * P:(m + 1) * P], xd[BC:BC + DTR, :],
                                     start=True, stop=True, tile_position=(BC, 0)).then_inc(dt_ps, 1)

                def row_c(i, par, n):
                    nc.tensor.matmul(psum[:, bank(n), :], sel[:, DS + n, :], bc[par][:, :], start=True, stop=True).then_inc(c_ps, 1)

                def row_b(i, par, n):
                    pe.wait_ge(c_sb, DS * i + n + 1)
                    nc.tensor.matmul(psum[:, bank(n), :], sel[:, n, :], bc[par][:, :], start=True, stop=True).then_inc(b_ps, 1)

                def add_other(i):
                    pe.wait_ge(y_in, 16 * (i + 1))
                    for m in range(DM):
                        nc.tensor.matmul(psum[:, m, :], ident[:, :], yi[:, m, :], start=True, stop=False).then_inc(y_added, 1)

                def sum_state(i, n, m):
                    k = n * DM + m
                    pe.wait_ge(hc_ready, HC0 + UNITS * i + k + 1)
                    nc.tensor.matmul(psum[:, m, :], ident[:, :], hc[:, k % GB, :], start=n == 0 and not reverse, stop=n == DS - 1
                                     ).then_inc(summed, 1)
                x_proj(0, 0, bank(1))
                for m in range(DM):
                    if m:
                        pe.wait_ge(dt_read, 2 * m)
                    dt_proj(0, m, bank(1))
                pe.wait_ge(dt_read, 2 * DM)
                pe.wait_ge(bc_mid, 1)
                pe.wait_ge(bc_low, 1)
                row_c(0, 0, 0)
                row_b(0, 0, 0)

                def step(i, par, pending, put_off):
                    def sum_before(n, m):
                        if n > 0:
                            sum_state(i, n - 1, m)
                        elif pending:
                            sum_state(i - 1, DS - 1, m)
                    for n in range(DS):
                        prepares = n == SLOT_X or SLOT_DT <= n < SLOT_DT + DM
                        ni, npar, nn = (i, par, n + 1) if n + 1 < DS else (i + 1, 1 - par, 0)
                        if nn == 0:
                            pe.wait_ge(bc_mid, ni + 1)
                            pe.wait_ge(bc_low, ni + 1)
                        pe.wait_ge(db_ready, UNITS * i + max(1, n * DM))
                        row_c(ni, npar, nn)
                        if n == 1:
                            row_b(ni, npar, nn)
                            pe.wait_ge(y_read, DM * i)
                            if reverse:
                                add_other(i)
                        sum_before(n, 0)
                        if n == SLOT_X:
                            pe.wait_ge(c_sb, DS * ni + nn + 1)
                            x_proj(i + 1, 1 - par, bank(nn))
                        if SLOT_DT <= n < SLOT_DT + DM:
                            pe.wait_ge(c_sb, DS * ni + nn + 1)
                            dt_proj(i + 1, n - SLOT_DT, bank(nn))
                        if prepares:
                            sum_before(n, 1)
                        if n == SLOT_X:
                            pe.wait_ge(xd_sb, i + 2)
                        if SLOT_DT <= n < SLOT_DT + DM:
                            pe.wait_ge(dt_read, 2 * (DM * (i + 1) + n - SLOT_DT + 1))
                        if n != 1:
                            row_b(ni, npar, nn)
                        for m in range(2 if prepares else 1, DM):
                            sum_before(n, m)
                    if not put_off:
                        for m in range(DM):
                            sum_state(i, DS - 1, m)
                in_steps(pe, step)

            @block.scalar
            def _(act):
                act.sem_inc(carried, CAR0)
                act.wait_ge(w_in, 112)
                nc.scalar.activation(an[:, :, :], al[:, :, :], ACT.Exp).then_inc(a_exp, 1)

                def prepare(i, par):
                    def first_tap(m):
                        act.wait_ge(win_in, 16 * (i + 1))
                        off = 2 * HALO if reverse else 0
                        nc.scalar.activation(cv[:, m, :], win[:, m, off:off + CH], ACT.Copy, scale=cw[:, m, 0:1]).then_inc(tap0, 1)

                    def silu(m):
                        act.wait_ge(taps, DM * HALO * i + 2 * HALO * (m // 2) + 2 * (HALO - 1) + m % 2 + 1)
                        nc.scalar.activation(u[par][:, m, :], cv[:, m, :], ACT.Silu, bias=cb[:, m:m + 1]).then_inc(u_ready, 1)

                    def split(at):
                        act.wait_ge(xp_ps, i + 1)
                        act.wait_ge(bc_rest, i)
                        nc.scalar.activation(xd[:, :], psum[0:BC + DTR, at, :], ACT.Copy).then_inc(xd_sb, 1)
                        act.wait_ge(xd_sb, i + 1)
                        nc.scalar.activation(bc[par][0:BC, :], xd[0:BC, :], ACT.Copy).then_inc(bc_high, 1)

                    def middle():
                        act.wait_ge(bc_rest, i + 1)
                        nc.scalar.activation(bc[par][BC:2 * BC, :], rest[:, :], ACT.Copy).then_inc(bc_mid, 1)

                    def softplus_in(m, at):
                        act.wait_ge(dt_ps, DM * i + m + 1)
                        if m == 0:
                            act.wait_ge(dt_ready, DM * i)
                        nc.scalar.activation(sp1[:, m, :], psum[:, at, :], ACT.Abs, bias=tb[:, m:m + 1]).then_inc(dt_read, 1)
                        nc.scalar.activation(sp2[:, m, :], psum[:, at, :], ACT.Relu, bias=tb[:, m:m + 1]).then_inc(dt_read, 1)

                    def softplus_exp():
                        act.wait_ge(dt_read, 2 * DM * (i + 1))
                        nc.scalar.activation(sp1[:, :, :], sp1[:, :, :], ACT.Exp, scale=-1.0).then_inc(logs, 1)

                    def softplus_ln():
                        act.wait_ge(logs, 2 * i + 1)
                        nc.scalar.activation(sp1[:, :, :], sp1[:, :, :], ACT.Ln, bias=1.0).then_inc(logs, 1)
                    return first_tap, silu, split, middle, softplus_in, softplus_exp, softplus_ln

                def row_c(i, n):
                    act.wait_ge(c_ps, DS * i + n + 1)
                    act.wait_ge(hc_ready, HC0 + UNITS * i + DM * (n - CB + 1))
                    nc.scalar.activation(cs[:, n % CB, :], psum[:, bank(n), :], ACT.Copy).then_inc(c_sb, 1)

                first_tap, silu, split, middle, softplus_in, softplus_exp, softplus_ln = prepare(0, 0)
                for m in range(DM):
                    first_tap(m)
                for m in range(DM):
                    silu(m)
                split(bank(1))
                middle()
                for m in range(DM):
                    softplus_in(m, bank(1))
                softplus_exp()
                softplus_ln()
                row_c(0, 0)
                act.wait_ge(a_neg, 1)

                def step(i, par, pending, put_off):
                    first_tap, silu, split, middle, softplus_in, softplus_exp, softplus_ln = prepare(i + 1, 1 - par)
                    act.wait_ge(dt_ready, DM * (i + 1))

                    def carry(k):
                        act.wait_ge(scanned, UNITS * i + k + 1)
                        nc.scalar.activation(state[:, k:k + 1], h[:, k % HB, LAST:LAST + 1], ACT.Copy).then_inc(carried, 1)
                    for k, (n, m) in enumerate(UNIT):
                        if k >= 2:
                            act.wait_ge(scanned, UNITS * i + k - 1)
                        elif k == 0:
                            act.wait_ge(scanned, UNITS * i)
                        nc.scalar.activation(psum[:, BANK_A + k % 2, :], dt[par][:, m, :], ACT.Exp,
                                             scale=an[:, m, n:n + 1]).then_inc(decay, 1)
                        if m == 0:
                            row_c(*((i, n + 1) if n + 1 < DS else (i + 1, 0)))
                        if k >= 2:
                            carry(k - 2)
                        if k < DM:
                            first_tap(k)
                        if k == K_SILU:
                            for j in range(DM):
                                silu(j)
                        if k == DM * (SLOT_X + 1) - 1:
                            split(bank(SLOT_X + 1))
                        if k == DM * (SLOT_X + 1) + 1:
                            middle()
                        if SLOT_DT <= n < SLOT_DT + DM and m == 1:
                            softplus_in(n - SLOT_DT, bank(n + 1))
                        if k == K_EXP:
                            softplus_exp()
                        if k == K_LN:
                            softplus_ln()
                    carry(UNITS - 2)
                    carry(UNITS - 1)
                in_steps(act, step)

            @block.vector
            def _(dve):
                nc.vector.memset(sel[:, :, :], 0.0).then_inc(made, 1)
                dve.wait_ge(a_exp, 1)
                nc.vector.tensor_scalar(an[:, :, :], an[:, :, :], -1.0, None, ALU.mult).then_inc(a_neg, 1)
                dve.wait_ge(w_in, 112)

                def prepare(i, par):
                    def all_taps():
                        for pair in range(DM // 2):
                            for j in range(1, TAPS):
                                for m in (2 * pair, 2 * pair + 1):
                                    off = 2 * HALO - j if reverse else j
                                    if j == 1:
                                        dve.wait_ge(tap0, DM * i + m + 1)
                                    else:
                                        dve.wait_ge(taps, DM * HALO * i + 2 * HALO * pair + 2 * (j - 2) + m % 2 + 1)
                                    nc.vector.scalar_tensor_tensor(cv[:, m, :], win[:, m, off:off + CH], cw[:, m, j:j + 1],
                                                                   cv[:, m, :], ALU.mult, ALU.add).then_inc(taps, 1)

                    def split():
                        dve.wait_ge(bc_high, i + 1)
                        nc.vector.tensor_tensor(rest[:, :], xd[0:BC, :], bc[par][0:BC, :], ALU.subtract).then_inc(bc_rest, 1)
                        dve.wait_ge(bc_rest, i + 1)
                        nc.vector.tensor_copy(mid0[:, :], rest[:, :]).then_inc(made, 1)

                    def low():
                        dve.wait_ge(made, 4 + i + 1)
                        nc.vector.tensor_tensor(bc[par][2 * BC:3 * BC, :], rest[:, :], mid0[:, :], ALU.subtract).then_inc(bc_low, 1)

                    def softplus(m):
                        dve.wait_ge(logs, 2 * (i + 1))
                        nc.vector.tensor_tensor(dt[par][:, m, :], sp1[:, m, :], sp2[:, m, :], ALU.add).then_inc(dt_ready, 1)

                    return all_taps, split, low, softplus

                all_taps, split, low, softplus = prepare(0, 0)
                all_taps()
                split()
                low()
                for m in range(DM):
                    softplus(m)

                def start(b):
                    dve.wait_ge(carried, CAR0 + UNITS * NC * b)
                    nc.vector.memset(state[:, :], 0.0).then_inc(zeroed, 1)
                    hold(dve, zeroed, b + 1, dve_passed)

                def step(i, par, pending, put_off):
                    all_taps, split, low, softplus = prepare(i + 1, 1 - par)

                    def times_b(k):
                        n, m = UNIT[k]
                        dve.wait_ge(b_ps, DS * i + n + 1)
                        if k < DM:
                            dve.wait_ge(du_ready, DM * (i + 1))
                        if k >= DB:
                            dve.wait_ge(scanned, UNITS * i + k - DB + 1)
                        elif k == 0:
                            dve.wait_ge(scanned, UNITS * i)
                        nc.vector.tensor_tensor(db[:, k % DB, :], du[par][:, m, :], psum[:, bank(n), :], ALU.mult).then_inc(db_ready, 1)
                    times_b(0)
                    made_b = 1
                    for k in range(UNITS):
                        for j in range(made_b, min(UNITS, k + 1 + (LOOKAHEAD if k == K_LN else 1))):
                            times_b(j)
                            made_b = j + 1
                        dve.wait_ge(decay, UNITS * i + k + 1)
                        dve.wait_ge(db_ready, UNITS * i + k + 1)
                        dve.wait_ge(carried, CAR0 + UNITS * i + k - HB + 1)
                        dve.wait_ge(hc_ready, HC0 + UNITS * i + k - HB + 1)
                        nc.vector.tensor_tensor_scan(h[:, k % HB, flip], psum[:, BANK_A + k % 2, flip], db[:, k % DB, flip],
                                                     state[:, k:k + 1], ALU.mult, ALU.add).then_inc(scanned, 1)
                        if pending and k == K_Y:
                            finish(i - 1, 1 - par)
                        if k == K_TAPS:
                            all_taps()
                        if k == DM * (SLOT_X + 1) - 1:
                            split()
                        if k == DM * (SLOT_X + 1) + 1:
                            low()
                        if K_SOFT <= k < K_SOFT + DM:
                            softplus(k - K_SOFT)
                    if not put_off:
                        finish(i, par)

                def finish(i, par):
                    for m in range(DM):
                        dve.wait_ge(summed, SUM0 + UNITS * i + UNITS - DM + m + 1)
                        dve.wait_ge(stored, 16 * i)
                        nc.vector.scalar_tensor_tensor((yt if reverse else yo)[:, m, :], u[par][:, m, :], dw[:, m:m + 1],
                                                       psum[:, m, :], ALU.mult, ALU.add).then_inc(y_read, 1)
                    if reverse:
                        dve.wait_ge(z_in, 16 * (i + 1))
                        for m in range(DM):
                            dve.wait_ge(y_read, DM * i + m + 1)
                            nc.vector.tensor_tensor(yo[:, m, :], yt[:, m, :], zi[:, m, :], ALU.mult).then_inc(y_ready, 1)
                in_steps(dve, step, start)


def mamba_out(nc, tag, psum, y_in, base, x_out, outT, n_chunks):
    with Phase(nc, tag) as ph:
        sb, sem = ph.sb, ph.sem
        ys = [sb(f"ys{p}", [P, DM, CH]) for p in range(2)]
        bs = [sb(f"bs{p}", [P, TT, C]) for p in range(2)]
        res = sb("res", [P, TT, C])
        wo = sb("wo", [P, DM, C])
        w_in, loaded = sem("w_in"), [sem("loaded_even"), sem("loaded_odd")]
        o_ps, added, stored = sem("o_ps"), sem("added"), sem("stored")

        def phase_steps(eng, step):
            with eng.Fori(0, n_chunks // 2) as j:
                for par in range(2):
                    step(j * 2 + par, par)

        with nc.Block() as block:
            @block.sync
            def _(sp):
                def load(i, par, at):
                    sp.dma_start(ys[par][:, :, :], cols(y_in, at)).then_inc(loaded[par], 16)
                    sp.dma_start(bs[par][:, :, :], rows(base, at)).then_inc(loaded[par], 16)
                load(0, 0, 0)
                load(1, 1, 1)
                sp.dma_start(wo[:, :, :], outT.rearrange("(m p) n -> p m n", p=P)).then_inc(w_in, 16)

                def step(i, par):
                    sp.wait_ge(added, 2 * (i + 1))
                    sp.dma_start(rows(x_out, i), res[:, :, :]).then_inc(stored, 16)
                    load(i + 2, par, (i + 2) % n_chunks)
                phase_steps(sp, step)
                sp.wait_ge(stored, 16 * n_chunks)
                for par in range(2):
                    sp.wait_ge(loaded[par], 32 * (n_chunks // 2 + 1))

            @block.tensor
            def _(pe):
                pe.wait_ge(w_in, 16)

                def step(i, par):
                    pe.wait_ge(loaded[par], 32 * (i // 2 + 1))
                    pe.wait_ge(added, 2 * i)
                    for t in range(TT):
                        for m in range(DM):
                            ins = nc.tensor.matmul(psum[:, 2 * par + t // 2, (t % 2) * C:(t % 2 + 1) * C],
                                                   ys[par][:, m, t * P:(t + 1) * P], wo[:, m, :], start=m == 0, stop=m == DM - 1)
                        if t % 2:
                            ins.then_inc(o_ps, 1)
                phase_steps(pe, step)

            @block.vector
            def _(dve):
                def step(i, par):
                    dve.wait_ge(stored, 16 * i)
                    dve.wait_ge(loaded[par], 32 * (i // 2 + 1))
                    for n in range(2):
                        dve.wait_ge(o_ps, 2 * i + n + 1)
                        nc.vector.tensor_tensor(res[:, 2 * n:2 * n + 2, :],
                                                psum[:, 2 * par + n, :].rearrange("p (t c) -> p t c", t=2),
                                                bs[par][:, 2 * n:2 * n + 2, :], ALU.add).then_inc(added, 1)
                phase_steps(dve, step)


def macaron_block(nc, x, out, f, m, B, S):
    NT, N = B * S, B * S // CH
    scratch = lambda name, shape, dtype=F32: nc.dram_tensor(name, shape, dtype, kind="Internal").ap()
    t = scratch("t", (NT, C))
    qp = scratch("q_parts", (B * HEADS, 3, HD, S), BF16)
    kp = scratch("k_parts", (B * KVH, 3, HD, S), BF16)
    v = scratch("v", (B * KVH, S, HD))
    ao = scratch("ao", (NT, C))
    x1, x2 = scratch("x1", (NT, C)), scratch("x2", (NT, C))
    base = scratch("base", (NT, C))
    xp = scratch("xp", (DI, B, S + 2 * HALO))
    zs, y, yz = (scratch(n, (DI, NT)) for n in ("zs", "y", "yz"))
    with ExitStack() as ctx:
        psum = ctx.enter_context(nc.psum_tensor("psum", [P, 8, CH], F32))
        ident = ctx.enter_context(nc.sbuf_tensor("ident", [P, P], F32))

        def ffn(tag, x_in, x_out):
            ffn_in(nc, f"{tag}_in", psum, ident, x_in, t, qp, kp, v, f["norm1"], f["wqT"], f["wkT"], f["wvT"], B, S)
            attention(nc, f"{tag}_att", psum, ident, qp, kp, v, ao, B, S)
            ffn_out(nc, f"{tag}_out", psum, ident, ao, t, x_in, x_out, f["norm2"], f["woT"], f["gateT"], f["expT"], N)

        make_constants(nc, ident)
        ffn("ffn1", x, x1)
        mamba_in(nc, "mamba_in", psum, ident, x1, base, xp, zs, m["norm_w"], m["norm_b"], m["inT"], B, S)
        for tag, reverse, other, to in (("f", False, None, y), ("r", True, y, yz)):
            mamba_scan(nc, f"scan_{tag}", psum, ident, reverse, xp, zs, other, to, *(m[f"{n}_{tag}"] for n in
                       ("conv_w", "conv_b", "xprojT", "dtT", "dt_b", "a_log", "d")), B, S)
        mamba_out(nc, "mamba_out", psum, yz, base, x2, m["outT"], N)
        ffn("ffn2", x2, out)


def kernel(**inputs):
    import numpy as np
    import concourse.bacc as bacc
    from concourse.bass_utils import run_bass_kernel_spmd

    a = {k: np.asarray(v) for k, v in inputs.items()}
    B, S, _ = a["L0_attn_x"].shape
    turned = lambda w: np.ascontiguousarray(np.swapaxes(w, -1, -2))
    column = lambda w: np.ascontiguousarray(w.reshape(-1, P).T)
    tiles = lambda w: np.ascontiguousarray(w.reshape(-1, P, w.shape[-1]).swapaxes(0, 1))
    data = {"x": np.ascontiguousarray(a["L0_attn_x"].reshape(B * S, C))}
    ffn = {"norm1": column(a["L0_ffn_attn_norm_w"]), "norm2": column(a["L0_ffn_ffn_norm_w"]),
           "wqT": turned(a["L0_ffn_wq"]), "wkT": turned(a["L0_ffn_wk"]), "wvT": turned(a["L0_ffn_wv"]),
           "woT": turned(a["L0_ffn_wo"]), "gateT": turned(a["L0_ffn_gate_w"]), "expT": turned(a["L0_ffn_expert_w"])}
    mamba = {"norm_w": column(a["L0_attn_norm_w"]), "norm_b": column(a["L0_attn_norm_b"]),
             "inT": turned(a["L0_attn_in_proj_w"]), "outT": turned(a["L0_attn_out_proj_w"])}
    for d in "fr":
        xproj = a[f"L0_attn_x_proj_w_{d}"]
        mamba |= {
            f"conv_w_{d}": tiles(a[f"L0_attn_conv_w_{d}"].reshape(DI, TAPS)), f"conv_b_{d}": column(a[f"L0_attn_conv_b_{d}"]),
            f"xprojT_{d}": turned(np.concatenate([xproj[DTR:], xproj[:DTR]])),
            f"dtT_{d}": turned(a[f"L0_attn_dt_proj_w_{d}"]), f"dt_b_{d}": column(a[f"L0_attn_dt_proj_b_{d}"]),
            f"a_log_{d}": tiles(a[f"L0_attn_A_log_{d}"]), f"d_{d}": column(a[f"L0_attn_D_{d}"])}
    nc = bacc.Bacc("TRN2", target_bir_lowering=False, num_devices=1)
    aps = {}
    for part, arrays in (("", data), ("f_", ffn), ("m_", mamba)):
        aps[part] = {k: nc.dram_tensor(f"in_{part}{k}", w.shape, mybir.dt.from_np(w.dtype), kind="ExternalInput").ap()
                     for k, w in arrays.items()}
    out = nc.dram_tensor("out", (B * S, C), F32, kind="ExternalOutput").ap()
    macaron_block(nc, aps[""]["x"], out, aps["f_"], aps["m_"], B, S)
    given = {f"in_{part}{k}": w for part, arrays in (("", data), ("f_", ffn), ("m_", mamba)) for k, w in arrays.items()}
    r = run_bass_kernel_spmd(nc, [given], core_ids=[0])
    return r.results[0]["out"].reshape(B, S, C)
```
